# Optimizing a Trainium2 kernel written in Bass

```python
import numpy as np
import jax
import jax.numpy as jnp

def _softmax(x, axis=-1):
    return jax.nn.softmax(x, axis=axis)

def _gelu(x):
    return jax.nn.gelu(x, approximate=True)

def _silu(x):
    return jax.nn.silu(x)

def _sigmoid(x):
    return jax.nn.sigmoid(x)

def _layernorm(x, axis=-1, eps=1e-05):
    m = jnp.mean(x, axis=axis, keepdims=True)
    v = jnp.var(x, axis=axis, keepdims=True)
    return (x - m) / jnp.sqrt(v + eps)

def _scatter_add(tgt, idx, src, axis=0):
    return tgt.at[idx].add(src)

def _segment_sum(src, seg, n):
    return jax.ops.segment_sum(src, seg, n)
kernel_name = 'mk_adaln_ffn_d2_seqx_r4_42fb34'

def setup_inputs(seed: int=0):
    np.random.seed(seed)
    _w = jnp.asarray

    def _rec_inputs():
        import jax
        import jax.numpy as jnp
        _rk = jax.random.key(seed)
        x = -0.000125 + 0.9999 * jax.random.normal(jax.random.fold_in(_rk, 1), (4, 512, 512), jnp.float32)
        _lenS = 512 - jax.random.randint(jax.random.fold_in(_rk, 7), (4,), 0, max(1, 512 // 4) + 1, jnp.int32)
        _lenS2 = 512 - jax.random.randint(jax.random.fold_in(_rk, 8), (4,), 0, max(1, 512 // 4) + 1, jnp.int32)
        fside_BxSxS_0 = -1.52775e-05 + 0.999936 * jax.random.normal(jax.random.fold_in(_rk, 11), (4, 512, 512), jnp.float32)
        cond_512 = -5.03954e-05 + 1.00559 * jax.random.normal(jax.random.fold_in(_rk, 12), (4, 128), jnp.float32)
        return (x, fside_BxSxS_0, cond_512)
    x, fside_BxSxS_0, cond_512 = _rec_inputs()

    def _L0_cond_setup():
        import jax, jax.numpy as jnp
        from jax import lax
        import numpy as np
        B, T, C, TD = (8, 512, 512, 128)

        def _bi_wkv(r, k, v, w, u, time_emb):
            tf = jax.nn.sigmoid(jnp.sum(time_emb, axis=-1))[:, None, None]
            decay = jnp.exp(-jnp.exp(w.astype(jnp.float32)))[None, :] * (0.5 + 0.5 * tf[:, :, 0])
            kf = k.astype(jnp.float32)
            vf = v.astype(jnp.float32)
            ek = jnp.exp(jnp.minimum(kf, 30.0))
            ekv = ek * vf

            def step(carry, x):
                a, b = carry
                ekv_t, ek_t = x
                a = a * decay + ekv_t
                b = b * decay + ek_t
                return ((a, b), (a, b))
            ekv_t = jnp.swapaxes(ekv, 0, 1)
            ek_t = jnp.swapaxes(ek, 0, 1)
            init = (jnp.zeros_like(decay), jnp.zeros_like(decay))
            _, (nf, df) = lax.scan(step, init, (ekv_t, ek_t))
            _, (nb, db) = lax.scan(step, init, (ekv_t, ek_t), reverse=True)
            nf = jnp.swapaxes(nf, 0, 1)
            df = jnp.swapaxes(df, 0, 1)
            nb = jnp.swapaxes(nb, 0, 1)
            db = jnp.swapaxes(db, 0, 1)
            euk = jnp.exp(jnp.minimum(u.astype(jnp.float32)[None, None, :] + kf, 30.0))
            num = nf + nb - ekv + euk * vf
            den = df + db - ek + euk
            base = jax.nn.sigmoid(r.astype(jnp.float32)) * (num / jnp.maximum(den, 1e-08))
            out = base * (0.8 + 0.2 * tf)
            return out.astype(r.dtype)
        key = jax.random.key(seed)
        ks = jax.random.split(key, 6)
        return {'r': jax.random.normal(ks[0], (B, T, C), dtype=jnp.float32), 'k': jax.random.normal(ks[1], (B, T, C), dtype=jnp.float32), 'v': jax.random.normal(ks[2], (B, T, C), dtype=jnp.float32), 'w': jax.random.normal(ks[3], (C,), dtype=jnp.float32), 'u': jax.random.normal(ks[4], (C,), dtype=jnp.float32), 'time_emb': jax.random.normal(ks[5], (B, TD), dtype=jnp.float32)}
    _L0_cond_all = _L0_cond_setup()
    _L0_cond_in = {k: v for k, v in _L0_cond_all.items() if k in ('w', 'u')}
    del _L0_cond_all

    def _L0_ffn_setup():
        import jax, jax.numpy as jnp
        import numpy as np
        B_, S_, H_, O_ = (4, 512, 512, 512)
        E_, R_ = (8, 16)
        LORA_ALPHA = 16.0
        key = jax.random.key(seed)
        ks = jax.random.split(key, 5)
        x = jax.random.normal(ks[0], (B_, S_, H_), dtype=jnp.float32)
        W = jax.random.normal(ks[1], (O_, H_), dtype=jnp.float32) * 0.02
        gate_w = jax.random.normal(ks[2], (E_, H_), dtype=jnp.float32) * 0.02
        A = jax.random.normal(ks[3], (E_, R_, H_), dtype=jnp.float32) * 0.02
        B = jax.random.normal(ks[4], (E_, O_, R_), dtype=jnp.float32) * 0.02
        return {'x': x, 'W': W, 'gate_w': gate_w, 'A': A, 'B': B}
    _L0_ffn_all = _L0_ffn_setup()
    _L0_ffn_in = {k: v for k, v in _L0_ffn_all.items() if k in ('W', 'gate_w', 'A', 'B')}
    del _L0_ffn_all

    def _L1_cond_setup():
        import jax, jax.numpy as jnp
        from jax import lax
        import numpy as np
        B, T, C, TD = (8, 512, 512, 128)

        def _bi_wkv(r, k, v, w, u, time_emb):
            tf = jax.nn.sigmoid(jnp.sum(time_emb, axis=-1))[:, None, None]
            decay = jnp.exp(-jnp.exp(w.astype(jnp.float32)))[None, :] * (0.5 + 0.5 * tf[:, :, 0])
            kf = k.astype(jnp.float32)
            vf = v.astype(jnp.float32)
            ek = jnp.exp(jnp.minimum(kf, 30.0))
            ekv = ek * vf

            def step(carry, x):
                a, b = carry
                ekv_t, ek_t = x
                a = a * decay + ekv_t
                b = b * decay + ek_t
                return ((a, b), (a, b))
            ekv_t = jnp.swapaxes(ekv, 0, 1)
            ek_t = jnp.swapaxes(ek, 0, 1)
            init = (jnp.zeros_like(decay), jnp.zeros_like(decay))
            _, (nf, df) = lax.scan(step, init, (ekv_t, ek_t))
            _, (nb, db) = lax.scan(step, init, (ekv_t, ek_t), reverse=True)
            nf = jnp.swapaxes(nf, 0, 1)
            df = jnp.swapaxes(df, 0, 1)
            nb = jnp.swapaxes(nb, 0, 1)
            db = jnp.swapaxes(db, 0, 1)
            euk = jnp.exp(jnp.minimum(u.astype(jnp.float32)[None, None, :] + kf, 30.0))
            num = nf + nb - ekv + euk * vf
            den = df + db - ek + euk
            base = jax.nn.sigmoid(r.astype(jnp.float32)) * (num / jnp.maximum(den, 1e-08))
            out = base * (0.8 + 0.2 * tf)
            return out.astype(r.dtype)
        key = jax.random.key(seed)
        ks = jax.random.split(key, 6)
        return {'r': jax.random.normal(ks[0], (B, T, C), dtype=jnp.float32), 'k': jax.random.normal(ks[1], (B, T, C), dtype=jnp.float32), 'v': jax.random.normal(ks[2], (B, T, C), dtype=jnp.float32), 'w': jax.random.normal(ks[3], (C,), dtype=jnp.float32), 'u': jax.random.normal(ks[4], (C,), dtype=jnp.float32), 'time_emb': jax.random.normal(ks[5], (B, TD), dtype=jnp.float32)}
    _L1_cond_all = _L1_cond_setup()
    _L1_cond_in = {k: v for k, v in _L1_cond_all.items() if k in ('w', 'u')}
    del _L1_cond_all

    def _L1_ffn_setup():
        import jax, jax.numpy as jnp
        import numpy as np
        IN_F, OUT_F = (512, 512)
        N_EXPERTS, RANK, TOP_K = (8, 128, 2)
        key = jax.random.key(seed)
        k_x, k_r, k_a, k_b = jax.random.split(key, 4)
        hidden_states = jax.random.normal(k_x, (4, 1024, IN_F), dtype=jnp.float32)
        router_w = jax.random.normal(k_r, (IN_F, N_EXPERTS), dtype=jnp.float32) * IN_F ** (-0.5)
        Wa = jax.random.normal(k_a, (N_EXPERTS, IN_F, RANK), dtype=jnp.float32) * IN_F ** (-0.5)
        Wb = jax.random.normal(k_b, (N_EXPERTS, RANK, OUT_F), dtype=jnp.float32) * RANK ** (-0.5)
        return {'hidden_states': hidden_states, 'router_w': router_w, 'Wa': Wa, 'Wb': Wb}
    _L1_ffn_all = _L1_ffn_setup()
    _L1_ffn_in = {k: v for k, v in _L1_ffn_all.items() if k in ('router_w', 'Wa', 'Wb')}
    del _L1_ffn_all
    return {'x': x, 'fside_BxSxS_0': fside_BxSxS_0, 'cond_512': cond_512, 'L0_cond_w': _L0_cond_in['w'], 'L0_cond_u': _L0_cond_in['u'], 'L0_ffn_W': _L0_ffn_in['W'], 'L0_ffn_gate_w': _L0_ffn_in['gate_w'], 'L0_ffn_A': _L0_ffn_in['A'], 'L0_ffn_B': _L0_ffn_in['B'], 'L1_cond_w': _L1_cond_in['w'], 'L1_cond_u': _L1_cond_in['u'], 'L1_ffn_router_w': _L1_ffn_in['router_w'], 'L1_ffn_Wa': _L1_ffn_in['Wa'], 'L1_ffn_Wb': _L1_ffn_in['Wb']}

def reference(x, fside_BxSxS_0, cond_512, L0_cond_w, L0_cond_u, L0_ffn_W, L0_ffn_gate_w, L0_ffn_A, L0_ffn_B, L1_cond_w, L1_cond_u, L1_ffn_router_w, L1_ffn_Wa, L1_ffn_Wb):
    import jax
    import jax.numpy as jnp

    def _L0_cond_ref(r, k, v, w, u, time_emb):
        import jax, jax.numpy as jnp
        from jax import lax
        import numpy as np
        B, T, C, TD = (8, 512, 512, 128)

        def _bi_wkv(r, k, v, w, u, time_emb):
            tf = jax.nn.sigmoid(jnp.sum(time_emb, axis=-1))[:, None, None]
            decay = jnp.exp(-jnp.exp(w.astype(jnp.float32)))[None, :] * (0.5 + 0.5 * tf[:, :, 0])
            kf = k.astype(jnp.float32)
            vf = v.astype(jnp.float32)
            ek = jnp.exp(jnp.minimum(kf, 30.0))
            ekv = ek * vf

            def step(carry, x):
                a, b = carry
                ekv_t, ek_t = x
                a = a * decay + ekv_t
                b = b * decay + ek_t
                return ((a, b), (a, b))
            ekv_t = jnp.swapaxes(ekv, 0, 1)
            ek_t = jnp.swapaxes(ek, 0, 1)
            init = (jnp.zeros_like(decay), jnp.zeros_like(decay))
            _, (nf, df) = lax.scan(step, init, (ekv_t, ek_t))
            _, (nb, db) = lax.scan(step, init, (ekv_t, ek_t), reverse=True)
            nf = jnp.swapaxes(nf, 0, 1)
            df = jnp.swapaxes(df, 0, 1)
            nb = jnp.swapaxes(nb, 0, 1)
            db = jnp.swapaxes(db, 0, 1)
            euk = jnp.exp(jnp.minimum(u.astype(jnp.float32)[None, None, :] + kf, 30.0))
            num = nf + nb - ekv + euk * vf
            den = df + db - ek + euk
            base = jax.nn.sigmoid(r.astype(jnp.float32)) * (num / jnp.maximum(den, 1e-08))
            out = base * (0.8 + 0.2 * tf)
            return out.astype(r.dtype)
        return _bi_wkv(r, k, v, w, u, time_emb)

    def _L0_ffn_ref(x, W, gate_w, A, B):
        import jax, jax.numpy as jnp
        import numpy as np
        B_, S_, H_, O_ = (4, 512, 512, 512)
        E_, R_ = (8, 16)
        LORA_ALPHA = 16.0
        bsz, seq, hid = x.shape
        E = gate_w.shape[0]
        x_flat = x.reshape(-1, hid)
        out = x_flat @ W.T
        logits = x_flat @ gate_w.T
        probs = jax.nn.softmax(logits, axis=-1)
        topk_w, topk_idx = jax.lax.top_k(probs, 2)
        topk_w = topk_w / jnp.sum(topk_w, axis=-1, keepdims=True)
        onehot = jax.nn.one_hot(topk_idx, E, dtype=x.dtype)
        wmat = jnp.einsum('tk,tke->te', topk_w, onehot) * LORA_ALPHA
        h = jnp.einsum('th,erh->etr', x_flat, A)
        hw = h * wmat.T[:, :, None]
        lora = jnp.einsum('etr,eor->to', hw, B)
        return (out + lora).reshape(bsz, seq, -1)

    def _L1_cond_ref(r, k, v, w, u, time_emb):
        import jax, jax.numpy as jnp
        from jax import lax
        import numpy as np
        B, T, C, TD = (8, 512, 512, 128)

        def _bi_wkv(r, k, v, w, u, time_emb):
            tf = jax.nn.sigmoid(jnp.sum(time_emb, axis=-1))[:, None, None]
            decay = jnp.exp(-jnp.exp(w.astype(jnp.float32)))[None, :] * (0.5 + 0.5 * tf[:, :, 0])
            kf = k.astype(jnp.float32)
            vf = v.astype(jnp.float32)
            ek = jnp.exp(jnp.minimum(kf, 30.0))
            ekv = ek * vf

            def step(carry, x):
                a, b = carry
                ekv_t, ek_t = x
                a = a * decay + ekv_t
                b = b * decay + ek_t
                return ((a, b), (a, b))
            ekv_t = jnp.swapaxes(ekv, 0, 1)
            ek_t = jnp.swapaxes(ek, 0, 1)
            init = (jnp.zeros_like(decay), jnp.zeros_like(decay))
            _, (nf, df) = lax.scan(step, init, (ekv_t, ek_t))
            _, (nb, db) = lax.scan(step, init, (ekv_t, ek_t), reverse=True)
            nf = jnp.swapaxes(nf, 0, 1)
            df = jnp.swapaxes(df, 0, 1)
            nb = jnp.swapaxes(nb, 0, 1)
            db = jnp.swapaxes(db, 0, 1)
            euk = jnp.exp(jnp.minimum(u.astype(jnp.float32)[None, None, :] + kf, 30.0))
            num = nf + nb - ekv + euk * vf
            den = df + db - ek + euk
            base = jax.nn.sigmoid(r.astype(jnp.float32)) * (num / jnp.maximum(den, 1e-08))
            out = base * (0.8 + 0.2 * tf)
            return out.astype(r.dtype)
        return _bi_wkv(r, k, v, w, u, time_emb)

    def _L1_ffn_ref(hidden_states, router_w, Wa, Wb):
        import jax, jax.numpy as jnp
        import numpy as np
        IN_F, OUT_F = (512, 512)
        N_EXPERTS, RANK, TOP_K = (8, 128, 2)
        B, S, D = hidden_states.shape
        x = hidden_states.reshape(-1, D)
        norm = jnp.maximum(jnp.linalg.norm(x, axis=-1, keepdims=True), 1e-12)
        router_logits = x / norm @ router_w
        routing_weights = jax.nn.softmax(router_logits.astype(jnp.float32), axis=-1)
        rw, selected_experts = jax.lax.top_k(routing_weights, TOP_K)
        rw = rw / jnp.sum(rw, axis=-1, keepdims=True)
        rw = rw.astype(hidden_states.dtype)
        combine = jnp.sum(jax.nn.one_hot(selected_experts, N_EXPERTS, dtype=rw.dtype) * rw[..., None], axis=1)
        out = jnp.zeros((x.shape[0], OUT_F), dtype=hidden_states.dtype)
        for e in range(N_EXPERTS):
            out = out + combine[:, e, None] * (x @ Wa[e] @ Wb[e])
        return out.reshape(B, S, OUT_F)
    x = x + _L0_ffn_ref(_L0_cond_ref(x, fside_BxSxS_0, fside_BxSxS_0, L0_cond_w, L0_cond_u, cond_512), L0_ffn_W, L0_ffn_gate_w, L0_ffn_A, L0_ffn_B)
    x = x + _L1_ffn_ref(_L1_cond_ref(x, fside_BxSxS_0, fside_BxSxS_0, L1_cond_w, L1_cond_u, cond_512), L1_ffn_router_w, L1_ffn_Wa, L1_ffn_Wb)
    return x

_drawn_inputs = setup_inputs


def setup_inputs(seed=0):
    import zlib

    import numpy as np

    out = dict(_drawn_inputs(seed))
    spreads = {}
    factors = {}
    for name, (base, spread) in spreads.items():
        noise = np.random.default_rng([zlib.crc32(name.encode()), seed]).standard_normal(out[name].shape)
        drawn = base * np.exp(spread * noise) if base else spread * noise
        out[name] = jnp.asarray(drawn.astype(out[name].dtype))
    for name, factor in factors.items():
        out[name] = (out[name] * factor).astype(out[name].dtype)
    return out
```

```python
from contextlib import ExitStack
from math import log

import concourse.bass as bass
from concourse import mybir

F32 = mybir.dt.float32
F32R = mybir.dt.float32r
U32 = mybir.dt.uint32
ALU = mybir.AluOpType
ACT = mybir.ActivationFunctionType
AX = mybir.AxisListType

P = 128
B, T, C = 4, 512, 512
CT = C // P
TT = T // P
NE = 8
RANK0 = 16
ALPHA = 16.0
CLAMP = 30.0
DEN_MIN = 1e-8
X_MIN = -43.0
LN_TINY = 2.0 ** -63
NORM_MIN = 1e-12
SS_SCALE = 2.0 ** 20
SMALL = 10


def build(nc, xT, kT, cond, wu_dram, w_ffn0, gate0, lora_a, lora_b, router1, wa1, wb1, out,
          comb_dram):
    with ExitStack() as ctx:
        def sb(name, shape, dt=F32):
            return ctx.enter_context(nc.sbuf_tensor(name, shape, dt))

        def sem(name):
            return ctx.enter_context(nc.semaphore(name))

        x_sb = sb("x_sb", [P, B * CT * T])
        k_sb = sb("k_sb", [P, CT, T])
        cond0 = sb("cond0", [P, CT, T])
        cond1 = sb("cond1", [P, CT, T])
        cond1_hi = sb("cond1_hi", [P, CT, T], F32R)
        cond1_lo = sb("cond1_lo", [P, CT, T], F32R)
        wffn = sb("wffn", [P, CT, C])
        wgate = sb("wgate", [P, CT, NE])
        wrouter = sb("wrouter", [P, CT, NE])
        wlora_a = sb("wlora_a", [P, CT, P])
        wlora_b = sb("wlora_b", [P, C])
        wa_hi = sb("wa_hi", [P, NE, CT, P], F32R)
        wa_lo = sb("wa_lo", [P, NE, CT, P], F32R)
        wb_hi = sb("wb_hi", [P, NE, C], F32R)
        wb_lo = sb("wb_lo", [P, NE, C], F32R)
        eu = sb("eu", [P, CT, T])
        fd = sb("fd", [P, CT, T])
        fn = sb("fn", [P, CT, T])
        sig = sb("sig", [P, 2, T])
        lora_h = sb("lora_h", [P, T])
        ss = sb("ss", [P, T])
        combT = ss[0:NE, :]
        comb = sb("comb", [P, 4, T])
        hs = sb("hs", [P, 2, T])
        hs_hi = sb("hs_hi", [P, 2, T], F32R)
        hs_lo = sb("hs_lo", [P, 2, T], F32R)
        ident = sb("ident", [P, P])
        ones = sb("ones", [P, 2])
        iota = sb("iota", [P, TT, 2, NE])
        wu = sb("wu", [P, 2, 2, CT])
        dec = sb("dec", [P, B * 2 * CT])
        omd2 = sb("omd2", [P, B * 2 * CT])
        omd2_now = sb("omd2_now", [P, 2 * CT])
        gain_now = sb("gain_now", [P, 2])
        om = sb("om", [P, B * 2 * CT])
        tf = sb("tf", [P, B])
        half = sb("half", [P, B])
        ln_gain = sb("ln_gain", [P, B])
        lntiny = sb("lntiny", [P, 2])
        lg = sb("lg", [P, TT, NE])
        mx_ready = sb("mx_ready", [P, 1])
        mx = sb("mx", [P, TT, 8])
        mi = sb("mi", [P, TT, 8], U32)
        idxf = sb("idxf", [P, TT, 2])
        oh = sb("oh", [P, TT, 2, NE])
        dlt = sb("dlt", [P, TT])
        edl = sb("edl", [P, TT])
        den2 = sb("den2", [P, TT])
        rec2 = sb("rec2", [P, TT])
        wp = sb("wp", [P, TT, 2])
        cw = sb("cw", [P, TT, NE])
        rn = sb("rn", [P, TT])

        acc = ctx.enter_context(nc.psum_tensor("acc", [P, 4, T], F32))
        hb = ctx.enter_context(nc.psum_tensor("hb", [P, 3, T], F32))
        mis = ctx.enter_context(nc.psum_tensor("mis", [P, T], F32))
        lgp = [mis[:, 0:32].rearrange("p (t e) -> p t e", t=TT), mis[:, 32:64].rearrange("p (t e) -> p t e", t=TT)]
        ssp = mis[:, 64:64 + TT]
        stage = x_sb[:, 2 * CT * T:4 * CT * T]
        cond_bc = comb[:, 0, :]

        x_in, c_in, wu_in, wf_in, wg_in = sem("x_in"), sem("c_in"), sem("wu_in"), sem("wf_in"), sem("wg_in")
        raw_in = sem("raw_in")
        k_in = [sem(f"k_in{i}") for i in range(CT)]
        comb_in = [sem(f"comb_in{i}") for i in range(4)]
        comb_out, y_out = sem("comb_out"), sem("y_out")
        consts_done, setup_v, setup_a, decay_done, now_done = (sem(n) for n in ("consts_done", "setup_v", "setup_a", "decay_done", "now_done"))
        kc_done, fwd_done, bwd_done, den_done, ratio_done = (sem(n) for n in ("kc_done", "fwd_done", "bwd_done", "den_done", "ratio_done"))
        exp_done, scaled_done, lnd_done, y_done = (sem(n) for n in ("exp_done", "scaled_done", "lnd_done", "y_done"))
        ekv_done, g_done, num_done = sem("ekv_done"), sem("g_done"), sem("num_done")
        xc_done, sig_exp, sig_ln, sig_done, cond_done = (sem(n) for n in ("xc_done", "sig_exp", "sig_ln", "sig_done", "cond_done"))
        sq_steps, ss_done = sem("sq_steps"), sem("ss_done")
        logits_done, small, edl_done, cw_done = sem("logits_done"), sem("small"), sem("edl_done"), sem("cw_done")
        lnss_done, ssmax_done, rn_done = sem("lnss_done"), sem("ssmax_done"), sem("rn_done")
        lorah_done, wrep_done, wrep_evac, lorah_used = sem("lorah_done"), sem("wrep_done"), sem("wrep_evac"), sem("lorah_used")
        ffn0_done, acc_read, ct_done, ct_evac = sem("ffn0_done"), sem("acc_read"), sem("ct_done"), sem("ct_evac")
        h_done, hs_done, hi_done, lo_done, exp_out_done = (sem(n) for n in ("h_done", "hs_done", "hi_done", "lo_done", "exp_out_done"))
        ffn1_done = sem("ffn1_done")
        c1hi_done, c1lo_done = sem("c1hi_done"), sem("c1lo_done")
        whi_done, wlo_done = sem("whi_done"), sem("wlo_done")

        block = ctx.enter_context(nc.Block())

        def s_of(b, l, ct):
            return b * 8 + (4 * l + ct)

        def x_tile(b, ct):
            if isinstance(b, int):
                return x_sb[:, (b * CT + ct) * T:(b * CT + ct + 1) * T]
            return x_sb[:, bass.ds(b * (CT * T) + ct * T, T)]

        def col(t, b, l, ct):
            if isinstance(b, int):
                i = b * 8 + l * 4 + ct
                return t[:, i:i + 1]
            return t[:, bass.ds(b * 8 + (l * 4 + ct), 1)]

        def isint(b, n):
            return isinstance(b, int) and b == n

        def isfirst(b):
            return isint(b, 0)

        def x1_count(b, o):
            return o + 1 if isfirst(b) else b * 8 + (o - 3)

        def y_count(f, o):
            return 8 * f + o + 5 if isint(f, B - 1) else f * 8 + (o + 9)

        FIRST_TILES = [(0, 0, ct) for ct in range(CT)]

        def tiles_of(b, last):
            own = [(b, 1, ct) for ct in range(CT)]
            return own if last else own + [(b + 1, 0, ct) for ct in range(CT)]

        def turns(eng, turn):
            turn(0, True, False)
            with eng.Fori(1, B - 1) as b:
                turn(b, False, False)
            turn(B - 1, False, True)

        @block.sync
        def _(sp):
            sp.dma_start(cond_bc, cond.partition_broadcast(P)).then_inc(c_in, 16)
            sp.dma_start(wu[:], wu_dram).then_inc(wu_in, 16)
            for ct in range(CT):
                sp.dma_start(k_sb[:, ct, :], kT[0, ct]).then_inc(k_in[ct], 16)
            sp.dma_start(x_sb[:, 0:CT * T], xT[0]).then_inc(x_in, 16)
            sp.dma_start(wgate[:], gate0).then_inc(wf_in, 16)
            sp.dma_start(wlora_a[:], lora_a).then_inc(wf_in, 16)
            sp.dma_start(wffn[:], w_ffn0).then_inc(wf_in, 16)
            sp.dma_start(wlora_b[:], lora_b).then_inc(wf_in, 16)
            sp.dma_start(wrouter[:], router1).then_inc(wf_in, 16)
            sp.wait_ge(x_in, 16)
            sp.dma_start(x_sb[:, CT * T:2 * CT * T], xT[1]).then_inc(x_in, 16)
            sp.dma_start(stage, wa1).then_inc(raw_in, 16)

            def turn(b, first, last):
                if first:
                    sp.wait_ge(wlo_done, 1)
                    sp.dma_start(stage, wb1).then_inc(raw_in, 16)
                else:
                    sp.wait_ge(ct_evac, b)
                    sp.dma_start(comb_dram, combT).then_inc(comb_out, 16)
                    sp.wait_ge(comb_out, b * 16)
                    comb_loads(b - 1, 0)
                if not last:
                    for ct in range(CT):
                        sp.wait_ge(g_done, s_of(b, 1, ct) + 1)
                        sp.dma_start(k_sb[:, ct, :], k_row(b + 1, ct)).then_inc(k_in[ct], 16)
                if first:
                    sp.wait_ge(wlo_done, 2)
                    for n in (2, 3):
                        sp.wait_ge(x_in, 16 * n)
                        sp.dma_start(x_sb[:, n * CT * T:(n + 1) * CT * T], xT[n]).then_inc(x_in, 16)
                else:
                    comb_loads(b - 1, 4)
                    store(b - 1)

            def k_row(b, ct):
                return kT[b, ct] if isinstance(b, int) else kT[bass.ds(b, 1), ct].rearrange("a p t -> (a p) t")

            def comb_loads(f, e0):
                for e in range(e0, e0 + 4):
                    if e >= 4:
                        sp.wait_ge(hs_done, f * 8 + (e - 3))
                    else:
                        sp.wait_ge(acc_read, f * 8 + 4)
                    sp.dma_start(comb[:, e % 4, :], comb_dram[e, :].partition_broadcast(P)).then_inc(comb_in[e % 4], 16)

            def store(f):
                for o in range(CT):
                    sp.wait_ge(acc_read, y_count(f, o))
                    dst = out[f, :, o, :] if isinstance(f, int) else out[bass.ds(f, 1), :, o, :].rearrange("a p t -> (a p) t")
                    sp.dma_start(dst, x_tile(f, o)).then_inc(y_out, 16)

            turns(sp, turn)
            sp.wait_ge(ct_evac, B)
            sp.dma_start(comb_dram, combT).then_inc(comb_out, 16)
            sp.wait_ge(comb_out, B * 16)
            comb_loads(B - 1, 0)
            comb_loads(B - 1, 4)
            store(B - 1)
            sp.wait_ge(y_out, 16 * B * CT)

        @block.vector
        def _(dve):
            V = nc.vector

            dve.wait_ge(c_in, 16)
            V.tensor_reduce(tf[:], cond_bc.rearrange("p (b d) -> p b d", b=B), AX.X, ALU.add).then_inc(setup_v, 1)
            V.memset(lntiny[:, 0:1], LN_TINY).then_inc(setup_v, 1)
            V.memset(lntiny[:, 1:2], 0.5 * log(SS_SCALE)).then_inc(setup_v, 1)
            dve.wait_ge(setup_a, 3)
            V.tensor_scalar(half[:], tf[:], 1.0, None, ALU.add).then_inc(setup_v, 1)
            dve.wait_ge(setup_v, 4)
            V.reciprocal(tf[:], half[:]).then_inc(setup_v, 1)
            dve.wait_ge(setup_v, 5)
            V.tensor_scalar(half[:], tf[:], 0.5, 0.5, ALU.mult, ALU.add).then_inc(setup_v, 1)
            V.tensor_scalar(ln_gain[:], tf[:], 0.2, 0.8, ALU.mult, ALU.add).then_inc(setup_v, 1)
            dve.wait_ge(setup_v, 6)
            base = wu[:, 0].rearrange("p l c -> p (l c)")
            for b in range(B):
                V.tensor_scalar(dec[:, b * 8:b * 8 + 8], base, half[:, b:b + 1], None, ALU.mult).then_inc(setup_v, 1)
            dve.wait_ge(setup_v, 11)
            V.tensor_scalar(om[:], dec[:], -1.0, 1.0, ALU.mult, ALU.add).then_inc(setup_v, 1)
            dve.wait_ge(setup_v, 12)
            V.scalar_tensor_tensor(omd2[:], dec[:], 1.0, om[:], ALU.add, ALU.mult).then_inc(decay_done, 1)
            dve.wait_ge(decay_done, 1)

            def cut(tile):
                b, l, ct = tile
                dve.wait_ge(k_in[ct], b * 16 + 16)
                if not (isfirst(b) and l == 0):
                    dve.wait_ge(ratio_done, s_of(b, l, ct) - 3)
                V.tensor_scalar(fd[:, ct, :], k_sb[:, ct, :], CLAMP, None, ALU.min).then_inc(kc_done, 1)
                V.tensor_scalar(eu[:, ct, :], k_sb[:, ct, :], wu[:, 1, l, ct:ct + 1], CLAMP, ALU.add, ALU.min).then_inc(kc_done, 1)

            def forward(tile):
                b, l, ct = tile
                d = col(dec, b, l, ct).broadcast_to([P, T])
                dve.wait_ge(ekv_done, s_of(b, l, ct) + 1)
                for f in (fd, fn):
                    V.tensor_tensor_scan(f[:, ct, :], d, f[:, ct, :], 0.0, ALU.mult, ALU.add).then_inc(fwd_done, 1)

            def backward(tile):
                b, l, ct = tile
                s = s_of(b, l, ct)
                d = col(dec, b, l, ct).broadcast_to([P, T - 1])
                for n, f in enumerate((fd, fn)):
                    dve.wait_ge(scaled_done, s * 2 + (n + 1))
                    back = f[:, ct, 0:T - 1][:, ::-1]
                    V.tensor_tensor_scan(back, d, back, f[:, ct, T - 1:T], ALU.mult, ALU.add).then_inc(bwd_done, 1)
                dve.wait_ge(bwd_done, s * 2 + 1)
                dve.wait_ge(exp_done, s * 2 + 2)
                V.tensor_tensor(fd[:, ct, :], fd[:, ct, :], eu[:, ct, :], ALU.add).then_inc(den_done, 1)

            def ratio(tile):
                b, l, ct = tile
                s = s_of(b, l, ct)
                dve.wait_ge(y_done, s + 1)
                dve.wait_ge(num_done, s + 1)
                if l == 1 and not isfirst(b):
                    dve.wait_ge(c1lo_done, b * 4 + (ct - 3))
                    dve.wait_ge(logits_done, b * 2)
                dst = cond1[:, ct, :] if l else fn[:, ct, :]
                V.scalar_tensor_tensor(dst, fd[:, ct, :], 1.0 / DEN_MIN, fn[:, ct, :], ALU.min, ALU.mult).then_inc(ratio_done, 1)

            def cut_x(b, l, ct):
                if l == 0:
                    dve.wait_ge(x_in, b * 16 + 16)
                else:
                    dve.wait_ge(acc_read, x1_count(b, ct))
                if not (isfirst(b) and l == 0 and ct < 2):
                    dve.wait_ge(cond_done, s_of(b, l, ct) - 1)
                V.tensor_scalar(sig[:, ct % 2, :], x_tile(b, ct), X_MIN, None, ALU.max).then_inc(xc_done, 1)

            def condition(b, l, ct):
                s, r2 = s_of(b, l, ct), ct % 2
                dve.wait_ge(sig_done, s + 1)
                dve.wait_ge(ratio_done, s + 1)
                if l == 0:
                    if not isfirst(b):
                        dve.wait_ge(ffn0_done, b * 4)
                    V.tensor_tensor(cond0[:, ct, :], fn[:, ct, :], sig[:, r2, :], ALU.mult).then_inc(cond_done, 1)
                else:
                    V.tensor_tensor(cond1[:, ct, :], cond1[:, ct, :], sig[:, r2, :], ALU.mult).then_inc(cond_done, 1)

            def top2(b, l):
                z = b * 2 + l
                n0 = z * SMALL

                def sync_to(n):
                    dve.wait_ge(small, n0 + n)

                dve.wait_ge(logits_done, z + 1)
                if l == 0:
                    V.tensor_copy(lg[:], lgp[0]).then_inc(small, 1)
                else:
                    dve.wait_ge(lnss_done, b + 1)
                    V.tensor_scalar(rn[:], rn[:], log(NORM_MIN ** 2 * SS_SCALE), None, ALU.max).then_inc(ssmax_done, 1)
                    dve.wait_ge(rn_done, b + 1)
                    V.tensor_tensor(lg[:], lgp[1], rn[:].unsqueeze(2).broadcast_to([P, TT, NE]), ALU.mult).then_inc(small, 1)
                sync_to(1)
                V.memset(mx_ready[:], 0.0)
                for t in range(TT):
                    last = V.max(mx[:, t, :], lg[:, t, :])
                last.then_inc(small, 1)
                sync_to(2)
                V.tensor_tensor(dlt[:], mx[:, :, 1], mx[:, :, 0], ALU.subtract).then_inc(small, 1)
                for t in range(TT):
                    last = V.max_index(mi[:, t, :], mx[:, t, :], lg[:, t, :])
                last.then_inc(small, 1)
                sync_to(4)
                V.tensor_copy(idxf[:], mi[:, :, 0:2]).then_inc(small, 1)
                dve.wait_ge(edl_done, z + 1)
                V.tensor_scalar(den2[:], edl[:], 1.0, None, ALU.add).then_inc(small, 1)
                sync_to(5)
                dve.wait_ge(consts_done, 3 + NE)
                V.tensor_tensor(oh[:], iota[:], idxf[:].unsqueeze(3).broadcast_to([P, TT, 2, NE]), ALU.is_equal).then_inc(small, 1)
                sync_to(6)
                V.reciprocal(rec2[:], den2[:]).then_inc(small, 1)
                sync_to(8)
                gain = ALPHA if l == 0 else 1.0
                V.tensor_scalar(wp[:, :, 0], rec2[:], gain, None, ALU.mult)
                V.scalar_tensor_tensor(wp[:, :, 1], edl[:], gain, rec2[:], ALU.mult, ALU.mult).then_inc(small, 1)
                sync_to(9)
                V.tensor_tensor(oh[:], oh[:], wp[:].unsqueeze(3).broadcast_to([P, TT, 2, NE]), ALU.mult).then_inc(small, 1)
                sync_to(10)
                if l == 0:
                    wide = (oh[:, :, j, :].unsqueeze(3).broadcast_to([P, TT, NE, RANK0]) for j in range(2))
                    V.tensor_tensor(lora_h[:].rearrange("p (t e r) -> p t e r", t=TT, e=NE), *wide, ALU.add).then_inc(cw_done, 1)
                else:
                    V.tensor_tensor(cw[:], oh[:, :, 0, :], oh[:, :, 1, :], ALU.add).then_inc(cw_done, 1)

            def weigh_lora(b):
                dve.wait_ge(lorah_done, b + 1)
                dve.wait_ge(wrep_evac, b + 1)
                V.tensor_tensor(lora_h[:], hb[:, 0, :], lora_h[:], ALU.mult).then_inc(lorah_used, 1)

            def residual0(b):
                for o in range(CT):
                    dve.wait_ge(ffn0_done, b * 4 + (o + 1))
                    V.tensor_tensor(x_tile(b, o), acc[:, o, :], x_tile(b, o), ALU.add).then_inc(acc_read, 1)

            def weigh(f, e):
                n = f * 8 + e
                dve.wait_ge(h_done, n + 1)
                dve.wait_ge(comb_in[e % 4], f * 32 + (e // 4 * 16 + 16))
                if e >= 2:
                    dve.wait_ge(lo_done, n - 1)
                else:
                    dve.wait_ge(acc_read, f * 8 + 4)
                V.tensor_tensor(hs[:, e % 2, :], hb[:, e % 3, :], comb[:, e % 4, :], ALU.mult).then_inc(hs_done, 1)

            def residual1(f):
                for o in range(CT):
                    dve.wait_ge(ffn1_done, f * 4 + (o + 1))
                    V.tensor_tensor(x_tile(f, o), acc[:, o, :], x_tile(f, o), ALU.add).then_inc(acc_read, 1)

            def finish(tile):
                ratio(tile)
                if tile[1] == 0:
                    condition(*tile)

            def tick(n, tiles, finished=False):
                if 0 <= n + 1 < len(tiles):
                    cut(tiles[n + 1])
                if 0 <= n - 1 < len(tiles) and tiles[n - 1][1] == 0:
                    cut_x(*tiles[n - 1])
                if 0 <= n < len(tiles):
                    forward(tiles[n])
                if 0 <= n - 1 < len(tiles):
                    backward(tiles[n - 1])
                if 0 <= n - 2 < len(tiles) and not finished:
                    finish(tiles[n - 2])

            for n in range(-1, CT + 2):
                tick(n, FIRST_TILES)

            def turn(b, first, last):
                tiles = tiles_of(b, last)
                tick(-1, tiles)
                top2(b, 0)
                tick(0, tiles)
                tick(1, tiles)
                weigh_lora(b)
                tick(2, tiles)
                tick(3, tiles)
                residual0(b)
                cut_x(b, 1, 0)
                cut_x(b, 1, 1)
                tick(4, tiles)
                if not first:
                    weigh(b - 1, 0)
                condition(b, 1, 0)
                condition(b, 1, 1)
                cut_x(b, 1, 2)
                cut_x(b, 1, 3)
                if not first:
                    weigh(b - 1, 1)
                condition(b, 1, 2)
                finish(tiles[3])
                condition(b, 1, 3)
                tick(5, tiles, finished=True)
                for n in range(6, CT + CT + 2):
                    if not first:
                        weigh(b - 1, n - 4)
                    tick(n, tiles)
                if not first:
                    weigh(b - 1, 6)
                    weigh(b - 1, 7)
                    residual1(b - 1)
                top2(b, 1)

            turns(dve, turn)
            for e in range(NE):
                weigh(B - 1, e)
            residual1(B - 1)

        @block.scalar
        def _(act):
            A = nc.scalar.activation
            nc.scalar.preload_act_table_set("natural_log_exp_and_others")
            act.wait_ge(wu_in, 16)
            A(wu[:, 0], wu[:, 0], ACT.Exp).then_inc(setup_a, 1)
            act.wait_ge(setup_a, 1)
            A(wu[:, 0], wu[:, 0], ACT.Exp, scale=-1.0).then_inc(setup_a, 1)
            act.wait_ge(setup_v, 1)
            A(tf[:], tf[:], ACT.Exp, scale=-1.0).then_inc(setup_a, 1)

            def exps(tile):
                b, l, ct = tile
                for n, buf in enumerate((fd, eu)):
                    act.wait_ge(kc_done, s_of(b, l, ct) * 2 + (n + 1))
                    A(buf[:, ct, :], buf[:, ct, :], ACT.Exp).then_inc(exp_done, 1)

            def scale_of(b, l, ct):
                if isinstance(b, int):
                    return col(omd2, b, l, ct)
                return omd2_now[:, (1 - l) * CT + ct:(1 - l) * CT + ct + 1]

            def fetch_now(b):
                A(omd2_now[:], omd2[:, bass.ds(b * 8 + CT, 2 * CT)], ACT.Copy).then_inc(now_done, 1)
                A(gain_now[:], ln_gain[:, bass.ds(b, 2)], ACT.Copy).then_inc(now_done, 1)
                act.wait_ge(now_done, b * 2)

            def scale(tile):
                b, l, ct = tile
                for n, f in enumerate((fd, fn)):
                    act.wait_ge(fwd_done, s_of(b, l, ct) * 2 + (n + 1))
                    A(f[:, ct, 0:T - 1], f[:, ct, 0:T - 1], ACT.Copy, scale=scale_of(b, l, ct)).then_inc(scaled_done, 1)

            def log_den(tile):
                b, l, ct = tile
                act.wait_ge(den_done, s_of(b, l, ct) + 1)
                A(fd[:, ct, :], fd[:, ct, :], ACT.Ln, bias=lntiny[:, 0:1]).then_inc(lnd_done, 1)

            def inverse_den(tile):
                b, l, ct = tile
                act.wait_ge(lnd_done, s_of(b, l, ct) + 1)
                A(fd[:, ct, :], fd[:, ct, :], ACT.Exp, scale=-1.0).then_inc(y_done, 1)

            def sigmoid(tile, step):
                b, l, ct = tile
                s, buf = s_of(b, l, ct), sig[:, ct % 2, :]
                if step == 0:
                    act.wait_ge(xc_done, s + 1)
                    A(buf, buf, ACT.Exp, scale=-1.0).then_inc(sig_exp, 1)
                elif step == 1:
                    act.wait_ge(sig_exp, s + 1)
                    A(buf, buf, ACT.Ln, bias=1.0).then_inc(sig_ln, 1)
                else:
                    act.wait_ge(sig_ln, s + 1)
                    gain = ln_gain[:, b:b + 1] if isinstance(b, int) else gain_now[:, 1 - l:2 - l]
                    A(buf, buf, ACT.Exp, scale=-1.0, bias=gain).then_inc(sig_done, 1)

            def tick(n, tiles):
                if 0 <= n + 1 < len(tiles):
                    exps(tiles[n + 1])
                with_sig = 0 <= n - 1 < len(tiles) and tiles[n - 1][1] == 0
                if with_sig:
                    sigmoid(tiles[n - 1], 0)
                if 0 <= n < len(tiles):
                    scale(tiles[n])
                if with_sig:
                    sigmoid(tiles[n - 1], 1)
                if 0 <= n - 1 < len(tiles):
                    log_den(tiles[n - 1])
                if with_sig:
                    sigmoid(tiles[n - 1], 2)
                if 0 <= n - 1 < len(tiles):
                    inverse_den(tiles[n - 1])

            def edl_step(b, l):
                act.wait_ge(small, (b * 2 + l) * SMALL + 3)
                A(edl[:], dlt[:], ACT.Exp).then_inc(edl_done, 1)

            def split_hi(f, ct):
                act.wait_ge(acc_read, f * 8 + 4)
                act.wait_ge(cond_done, s_of(f, 1, ct) + 1)
                A(cond1_hi[:, ct, :], cond1[:, ct, :], ACT.Copy).then_inc(c1hi_done, 1)

            def hi_part(f, e):
                n = f * 8 + e
                act.wait_ge(hs_done, n + 1)
                if e >= 2:
                    act.wait_ge(exp_out_done, f * 7 + (e - 1))
                else:
                    act.wait_ge(acc_read, f * 8 + 4)
                A(hs_hi[:, e % 2, :], hs[:, e % 2, :], ACT.Copy).then_inc(hi_done, 1)

            def gates1(b):
                act.wait_ge(logits_done, b * 2 + 2)
                A(rn[:], ssp, ACT.Ln, scale=SS_SCALE, bias=lntiny[:, 0:1]).then_inc(lnss_done, 1)
                act.wait_ge(ssmax_done, b + 1)
                A(rn[:], rn[:], ACT.Exp, scale=-0.5, bias=lntiny[:, 1:2]).then_inc(rn_done, 1)
                edl_step(b, 1)

            def evac_combT(f):
                act.wait_ge(ct_done, f + 1)
                A(combT, hb[0:NE, 2, :], ACT.Copy).then_inc(ct_evac, 1)

            def weights_hi(which, c):
                act.wait_ge(raw_in, 16 * (which + 1))
                hi = (wa_hi[:].rearrange("p e k r -> p (e k r)"), wb_hi[:].rearrange("p e o -> p (e o)"))[which]
                A(hi[:, c * 1024:(c + 1) * 1024], stage[:, c * 1024:(c + 1) * 1024], ACT.Copy).then_inc(whi_done, 1)

            act.wait_ge(setup_v, 7)
            A(ln_gain[:], ln_gain[:], ACT.Ln).then_inc(setup_a, 1)
            act.wait_ge(setup_a, 4)
            act.wait_ge(decay_done, 1)
            for n in range(-1, CT + 2):
                tick(n, FIRST_TILES)

            def turn(b, first, last):
                tiles = tiles_of(b, last)
                if not first and not last:
                    fetch_now(b)
                tick(-1, tiles)
                edl_step(b, 0)
                if not first:
                    for ct in range(CT):
                        split_hi(b - 1, ct)
                tick(0, tiles)
                if not first:
                    evac_combT(b - 1)
                else:
                    for c in range(4):
                        weights_hi(0, c)
                tick(1, tiles)
                act.wait_ge(wrep_done, b + 1)
                A(lora_h[:], hb[:, 1, :], ACT.Copy).then_inc(wrep_evac, 1)
                tick(2, tiles)
                tick(3, tiles)
                for step in range(3):
                    for ct in range(2):
                        sigmoid((b, 1, ct), step)
                tick(4, tiles)
                if not first:
                    hi_part(b - 1, 0)
                for step in range(3):
                    for ct in range(2, 4):
                        sigmoid((b, 1, ct), step)
                if not first:
                    hi_part(b - 1, 1)
                tick(5, tiles)
                for n in range(6, CT + CT + 2):
                    if not first:
                        hi_part(b - 1, n - 4)
                    tick(n, tiles)
                    if first:
                        weights_hi(1, n - 6)
                if not first:
                    hi_part(b - 1, 6)
                    hi_part(b - 1, 7)
                gates1(b)

            turns(act, turn)
            for ct in range(CT):
                split_hi(B - 1, ct)
            evac_combT(B - 1)
            for e in range(NE):
                hi_part(B - 1, e)

        @block.gpsimd
        def _(pool):
            G = nc.gpsimd
            G.memset(ident[:], 0.0).then_inc(consts_done, 1)
            pool.wait_ge(consts_done, 1)
            G.affine_select(out=ident[:], in_=ident[:], compare_op=ALU.not_equal, fill=1.0, base=0,
                            pattern=[[-1, P]], channel_multiplier=1).then_inc(consts_done, 1)
            G.memset(ones[:], 1.0).then_inc(consts_done, 1)
            for e in range(NE):
                G.memset(iota[:, :, :, e:e + 1], float(e)).then_inc(consts_done, 1)

            def ekv_step(tile):
                b, l, ct = tile
                pool.wait_ge(exp_done, s_of(b, l, ct) * 2 + 1)
                G.tensor_tensor(fn[:, ct, :], fd[:, ct, :], k_sb[:, ct, :], ALU.mult).then_inc(ekv_done, 1)

            def numerator(tile):
                b, l, ct = tile
                s = s_of(b, l, ct)
                pool.wait_ge(den_done, s + 1)
                G.tensor_tensor(eu[:, ct, :], eu[:, ct, :], k_sb[:, ct, :], ALU.mult).then_inc(g_done, 1)
                pool.wait_ge(g_done, s + 1)
                pool.wait_ge(bwd_done, s * 2 + 2)
                G.tensor_tensor(fn[:, ct, :], fn[:, ct, :], eu[:, ct, :], ALU.add).then_inc(num_done, 1)

            def tick(n, tiles):
                if 0 <= n + 1 < len(tiles):
                    ekv_step(tiles[n + 1])
                if 0 <= n - 1 < len(tiles):
                    numerator(tiles[n - 1])

            def split_lo(f, ct):
                pool.wait_ge(c1hi_done, f * 4 + (ct + 1))
                G.tensor_tensor(cond1_lo[:, ct, :], cond1[:, ct, :], cond1_hi[:, ct, :].bitcast(F32), ALU.subtract).then_inc(c1lo_done, 1)

            def lo_part(f, e):
                n = f * 8 + e
                pool.wait_ge(hi_done, n + 1)
                G.tensor_tensor(hs_lo[:, e % 2, :], hs[:, e % 2, :], hs_hi[:, e % 2, :].bitcast(F32), ALU.subtract).then_inc(lo_done, 1)

            def squares(b, ct):
                pool.wait_ge(cond_done, s_of(b, 1, ct) + 1)
                n0 = b * 6
                if ct == 0:
                    if not isfirst(b):
                        pool.wait_ge(comb_out, b * 16)
                    G.tensor_tensor(ss[:], cond1[:, 0, :], cond1[:, 0, :], ALU.mult).then_inc(sq_steps, 1)
                    return
                if ct > 1:
                    pool.wait_ge(sq_steps, n0 + (2 * ct - 1))
                G.tensor_tensor(lora_h[:], cond1[:, ct, :], cond1[:, ct, :], ALU.mult).then_inc(sq_steps, 1)
                pool.wait_ge(sq_steps, n0 + 2 * ct)
                G.tensor_tensor(ss[:], ss[:], lora_h[:], ALU.add).then_inc(ss_done if ct == CT - 1 else sq_steps, 1)

            def weights_lo(which, c):
                pool.wait_ge(whi_done, which * 4 + c + 1)
                hi, lo = ((wa_hi, wa_lo), (wb_hi, wb_lo))[which]
                how = ("p e k r -> p (e k r)", "p e o -> p (e o)")[which]
                part = slice(c * 1024, (c + 1) * 1024)
                last = G.tensor_tensor(lo[:].rearrange(how)[:, part], stage[:, part],
                                       hi[:].rearrange(how)[:, part].bitcast(F32), ALU.subtract)
                if c == 3:
                    last.then_inc(wlo_done, 1)

            for n in range(-1, CT + 2):
                tick(n, FIRST_TILES)

            def turn(b, first, last):
                tiles = tiles_of(b, last)
                tick(-1, tiles)
                if not first:
                    split_lo(b - 1, 0)
                    split_lo(b - 1, 1)
                else:
                    weights_lo(0, 0)
                tick(0, tiles)
                if not first:
                    split_lo(b - 1, 2)
                else:
                    weights_lo(0, 1)
                tick(1, tiles)
                if not first:
                    split_lo(b - 1, 3)
                else:
                    weights_lo(0, 2)
                tick(2, tiles)
                if first:
                    weights_lo(0, 3)
                tick(3, tiles)
                tick(4, tiles)
                if not first:
                    lo_part(b - 1, 0)
                squares(b, 0)
                squares(b, 1)
                if not first:
                    lo_part(b - 1, 1)
                squares(b, 2)
                squares(b, 3)
                tick(5, tiles)
                for n in range(6, CT + CT + 2):
                    if not first:
                        lo_part(b - 1, n - 4)
                    tick(n, tiles)
                    if first:
                        weights_lo(1, n - 6)
                if not first:
                    lo_part(b - 1, 6)
                    lo_part(b - 1, 7)

            turns(pool, turn)
            for ct in range(CT):
                split_lo(B - 1, ct)
            for e in range(NE):
                lo_part(B - 1, e)

        @block.tensor
        def _(pe):
            MM = nc.tensor.matmul
            pe.wait_ge(wf_in, 16 * 5)
            pe.wait_ge(consts_done, 3 + NE)

            def gate0(b):
                pe.wait_ge(cond_done, s_of(b, 0, CT - 1) + 1)
                for k in range(CT):
                    mm = MM(hb[:, 0, :], wlora_a[:, k, :], cond0[:, k, :], start=k == 0, stop=k == CT - 1)
                mm.then_inc(lorah_done, 1)
                if not isfirst(b):
                    pe.wait_ge(small, b * 2 * SMALL - SMALL + 1)
                for t in range(TT):
                    for k in range(CT):
                        mm = MM(lgp[0][:, t, :], cond0[:, k, t * P:(t + 1) * P], wgate[:, k, :], start=k == 0, stop=k == CT - 1)
                mm.then_inc(logits_done, 1)

            def turn_comb(f):
                pe.wait_ge(cw_done, f * 2 + 2)
                for t in range(TT):
                    mm = MM(hb[0:NE, 2, t * P:(t + 1) * P], cw[:, t, :], ident[:], start=True, stop=True)
                mm.then_inc(ct_done, 1)

            def ffn0(b, first):
                for o in range(CT):
                    if o == 1:
                        pe.wait_ge(cw_done, b * 2 + 1)
                        for t in range(TT):
                            mm = MM(hb[:, 1, t * P:(t + 1) * P], lora_h[:, t * P:(t + 1) * P], ident[:], start=True, stop=True)
                        mm.then_inc(wrep_done, 1)
                    if not first:
                        pe.wait_ge(acc_read, b * 8 + (o - 7))
                    for k in range(CT):
                        MM(acc[:, o, :], wffn[:, k, o * P:(o + 1) * P], cond0[:, k, :], start=k == 0, stop=False)
                pe.wait_ge(lorah_used, b + 1)
                for o in range(CT):
                    MM(acc[:, o, :], wlora_b[:, o * P:(o + 1) * P], lora_h[:], start=False, stop=True).then_inc(ffn0_done, 1)

            def hidden(f, e):
                if e == 2:
                    pe.wait_ge(ct_evac, f + 1)
                n = 0
                for k in range(CT):
                    for w, c in ((wa_hi, cond1_hi), (wa_hi, cond1_lo), (wa_lo, cond1_hi)):
                        mm = MM(hb[:, e % 3, :], w[:, e, k, :], c[:, k, :], start=n == 0, stop=n == 3 * CT - 1)
                        n += 1
                mm.then_inc(h_done, 1)

            def expert_out(f, e):
                pe.wait_ge(lo_done, f * 8 + (e + 1))
                for o in range(CT):
                    if e == 0:
                        pe.wait_ge(acc_read, y_count(f - 1, o) if isint(f, B - 1) else x1_count(f + 1, o))
                    for n, (w, h) in enumerate(((wb_hi, hs_hi), (wb_hi, hs_lo), (wb_lo, hs_hi))):
                        mm = MM(acc[:, o, :], w[:, e, o * P:(o + 1) * P], h[:, e % 2, :], start=e == 0 and n == 0,
                                stop=e == NE - 1 and n == 2)
                    if e == NE - 1:
                        mm.then_inc(ffn1_done, 1)
                if e < NE - 1:
                    mm.then_inc(exp_out_done, 1)

            def ffn1(f):
                pe.wait_ge(c1lo_done, f * 4 + 4)
                if isinstance(f, int) and f == 0:
                    pe.wait_ge(wlo_done, 2)
                hidden(f, 0)
                hidden(f, 1)
                for e in range(NE):
                    if e + 2 < NE:
                        hidden(f, e + 2)
                    expert_out(f, e)

            def router1_step(b):
                pe.wait_ge(ss_done, b + 1)
                for t in range(TT):
                    for k in range(CT):
                        MM(lgp[1][:, t, :], cond1[:, k, t * P:(t + 1) * P], wrouter[:, k, :], start=k == 0, stop=k == CT - 1)
                for t in range(TT):
                    mm = MM(ssp[:, t:t + 1], ss[:, t * P:(t + 1) * P], ones[:, 0:1], start=True, stop=True)
                mm.then_inc(logits_done, 1)

            def turn(b, first, last):
                gate0(b)
                if not first:
                    turn_comb(b - 1)
                ffn0(b, first)
                if not first:
                    ffn1(b - 1)
                router1_step(b)

            turns(pe, turn)
            turn_comb(B - 1)
            ffn1(B - 1)


_SHAPES = {
    "xT": (B, P, CT, T), "kT": (B, CT, P, T), "cond": (1, B * P), "wu": (P, 2, 2, CT), "w_ffn0": (P, CT, C),
    "gate0": (P, CT, NE), "lora_a": (P, CT, P), "lora_b": (P, C), "router1": (P, CT, NE),
    "wa1": (P, NE * CT * P), "wb1": (P, NE * C),
}


def kernel(x, fside_BxSxS_0, cond_512, L0_cond_w, L0_cond_u, L0_ffn_W, L0_ffn_gate_w, L0_ffn_A, L0_ffn_B,
           L1_cond_w, L1_cond_u, L1_ffn_router_w, L1_ffn_Wa, L1_ffn_Wb):
    import numpy as np
    import concourse.bacc as bacc
    from concourse.bass_utils import run_bass_kernel_spmd

    def rows(w):
        return np.asarray(w).reshape(CT, P, -1).transpose(1, 0, 2)

    x, k = np.asarray(x), np.asarray(fside_BxSxS_0)
    wu = np.stack([np.asarray(a).reshape(CT, P) for a in (L0_cond_w, L1_cond_w, L0_cond_u, L1_cond_u)])
    data = {
        "xT": x.reshape(B, T, CT, P).transpose(0, 3, 2, 1),
        "kT": k.reshape(B, T, CT, P).transpose(0, 2, 3, 1),
        "cond": np.asarray(cond_512).reshape(1, B * P),
        "wu": wu.reshape(2, 2, CT, P).transpose(3, 0, 1, 2),
        "w_ffn0": rows(np.asarray(L0_ffn_W).T),
        "gate0": rows(np.asarray(L0_ffn_gate_w).T),
        "lora_a": rows(np.asarray(L0_ffn_A).reshape(P, C).T),
        "lora_b": np.asarray(L0_ffn_B).transpose(0, 2, 1).reshape(P, C),
        "router1": rows(L1_ffn_router_w),
        "wa1": np.asarray(L1_ffn_Wa).reshape(NE, CT, P, P).transpose(2, 0, 1, 3).reshape(P, -1),
        "wb1": np.asarray(L1_ffn_Wb).transpose(1, 0, 2).reshape(P, -1),
    }
    nc = bacc.Bacc("TRN2", target_bir_lowering=False, num_devices=1)
    arrays, args = {}, []
    for name, shape in _SHAPES.items():
        arrays[name + "_dram"] = np.ascontiguousarray(data[name])
        args.append(nc.dram_tensor(name + "_dram", shape, F32, kind="ExternalInput").ap())
    out = nc.dram_tensor("out_dram", (B, P, CT, T), F32, kind="ExternalOutput").ap()
    scratch = nc.dram_tensor("comb_dram", (NE, T), F32).ap()
    build(nc, *args, out, scratch)
    r = run_bass_kernel_spmd(nc, [arrays], core_ids=[0])
    got = np.asarray(r.results[0]["out_dram"])
    return np.ascontiguousarray(got.transpose(0, 3, 2, 1)).reshape(B, T, C)
```

```python
from contextlib import ExitStack
from math import log

import concourse.bass as bass
from concourse import mybir

F32 = mybir.dt.float32
F32R = mybir.dt.float32r
U32 = mybir.dt.uint32
ALU = mybir.AluOpType
ACT = mybir.ActivationFunctionType
AX = mybir.AxisListType

P = 128
B, T, C = 4, 512, 512
CT = C // P
TT = T // P
NE = 8
RANK0 = 16
ALPHA = 16.0
CLAMP = 30.0
DEN_MIN = 1e-8
X_MIN = -43.0
LN_TINY = 2.0 ** -63
NORM_MIN = 1e-12
SS_SCALE = 2.0 ** 20
SMALL = 10


def build(nc, xT, kT, cond, wu_dram, w_ffn0, gate0, lora_a, lora_b, router1, wa1, wb1, out,
          comb_dram):
    with ExitStack() as ctx:
        def sb(name, shape, dt=F32):
            return ctx.enter_context(nc.sbuf_tensor(name, shape, dt))

        def sem(name):
            return ctx.enter_context(nc.semaphore(name))

        x_sb = sb("x_sb", [P, B * CT * T])
        k_sb = sb("k_sb", [P, CT, T])
        cond0 = sb("cond0", [P, CT, T])
        cond1 = sb("cond1", [P, CT, T])
        cond1_hi = sb("cond1_hi", [P, CT, T], F32R)
        cond1_lo = sb("cond1_lo", [P, CT, T], F32R)
        wffn = sb("wffn", [P, CT, C])
        wgate = sb("wgate", [P, CT, NE])
        wrouter = sb("wrouter", [P, CT, NE])
        wlora_a = sb("wlora_a", [P, CT, P])
        wlora_b = sb("wlora_b", [P, C])
        wa_hi = sb("wa_hi", [P, NE, CT, P], F32R)
        wa_lo = sb("wa_lo", [P, NE, CT, P], F32R)
        wb_hi = sb("wb_hi", [P, NE, C], F32R)
        wb_lo = sb("wb_lo", [P, NE, C], F32R)
        eu = sb("eu", [P, CT, T])
        fd = sb("fd", [P, CT, T])
        fn = sb("fn", [P, CT, T])
        sig = sb("sig", [P, 2, T])
        lora_h = sb("lora_h", [P, T])
        sq = sb("sq", [P, T])
        ss = sb("ss", [P, T])
        combT = ss[0:NE, :]
        comb = sb("comb", [P, 4, T])
        hs = sb("hs", [P, 2, T])
        hs_hi = sb("hs_hi", [P, 2, T], F32R)
        hs_lo = sb("hs_lo", [P, 2, T], F32R)
        ident = sb("ident", [P, P])
        ones = sb("ones", [P, 2])
        iota = sb("iota", [P, TT, 2, NE])
        wu = sb("wu", [P, 2, 2, CT])
        dec = sb("dec", [P, B * 2 * CT])
        omd2 = sb("omd2", [P, B * 2 * CT])
        om = sb("om", [P, B * 2 * CT])
        tf = sb("tf", [P, B])
        half = sb("half", [P, B])
        ln_gain = sb("ln_gain", [P, B])
        lntiny = sb("lntiny", [P, 2])
        lg = sb("lg", [P, TT, NE])
        mx_ready = sb("mx_ready", [P, 1])
        mx = sb("mx", [P, TT, 8])
        mi = sb("mi", [P, TT, 8], U32)
        idxf = sb("idxf", [P, TT, 2])
        oh = sb("oh", [P, TT, 2, NE])
        dlt = sb("dlt", [P, TT])
        edl = sb("edl", [P, TT])
        den2 = sb("den2", [P, TT])
        rec2 = sb("rec2", [P, TT])
        wp = sb("wp", [P, TT, 2])
        cw = sb("cw", [P, TT, NE])
        rn = sb("rn", [P, TT])

        acc = ctx.enter_context(nc.psum_tensor("acc", [P, 4, T], F32))
        hb = ctx.enter_context(nc.psum_tensor("hb", [P, 3, T], F32))
        mis = ctx.enter_context(nc.psum_tensor("mis", [P, T], F32))
        lgp = [mis[:, 0:32].rearrange("p (t e) -> p t e", t=TT), mis[:, 32:64].rearrange("p (t e) -> p t e", t=TT)]
        ssp = mis[:, 64:64 + TT]
        stage = x_sb[:, 2 * CT * T:4 * CT * T]
        cond_bc = comb[:, 0, :]

        x_in, c_in, wu_in, wf_in, wg_in = sem("x_in"), sem("c_in"), sem("wu_in"), sem("wf_in"), sem("wg_in")
        raw_in = sem("raw_in")
        k_in = [sem(f"k_in{i}") for i in range(CT)]
        comb_in = [sem(f"comb_in{i}") for i in range(4)]
        comb_out, y_out = sem("comb_out"), sem("y_out")
        consts_done, setup_v, setup_a, decay_done = (sem(n) for n in ("consts_done", "setup_v", "setup_a", "decay_done"))
        kc_done, fwd_done, bwd_done, den_done, ratio_done = (sem(n) for n in ("kc_done", "fwd_done", "bwd_done", "den_done", "ratio_done"))
        exp_done, scaled_done, lnd_done, y_done = (sem(n) for n in ("exp_done", "scaled_done", "lnd_done", "y_done"))
        ekv_done, g_done, num_done = sem("ekv_done"), sem("g_done"), sem("num_done")
        xc_done, sig_exp, sig_ln, sig_done = (sem(n) for n in ("xc_done", "sig_exp", "sig_ln", "sig_done"))
        cond_done = [sem("cond0_done"), sem("cond1_done")]
        sq_steps, ss_done = sem("sq_steps"), sem("ss_done")
        logits_done, small, edl_done, cw_done = sem("logits_done"), sem("small"), sem("edl_done"), sem("cw_done")
        lnss_done, ssmax_done, rn_done = sem("lnss_done"), sem("ssmax_done"), sem("rn_done")
        lorah_done, cond0_used, wrep_done, wrep_evac, lorah_used = sem("lorah_done"), sem("cond0_used"), sem("wrep_done"), sem("wrep_evac"), sem("lorah_used")
        ffn0_done, acc_read, ct_done, ct_evac = sem("ffn0_done"), sem("acc_read"), sem("ct_done"), sem("ct_evac")
        h_done, hs_done, hi_done, lo_done, exp_out_done = (sem(n) for n in ("h_done", "hs_done", "hi_done", "lo_done", "exp_out_done"))
        ffn1_done = sem("ffn1_done")
        c1hi_done, c1lo_done = sem("c1hi_done"), sem("c1lo_done")
        whi_done, wlo_done = sem("whi_done"), sem("wlo_done")

        block = ctx.enter_context(nc.Block())

        GROUPS = [(0, 0), (1, 0), (0, 1), (2, 0), (1, 1), (3, 0), (2, 1), (3, 1)]

        def group(b, l):
            return GROUPS.index((b, l))

        def s_of(b, l, ct):
            return group(b, l) * CT + ct

        ACC = [(0, 0), (1, 0), (0, 1), (2, 0), (1, 1), (3, 0), (2, 1), (3, 1)]

        def acc_count(b, l, o):
            return ACC.index((b, l)) * CT + o + 1

        def acc_before(b, l, o):
            return acc_count(b, l, o) - CT

        def x_tile(b, ct):
            return x_sb[:, (b * CT + ct) * T:(b * CT + ct + 1) * T]

        def col(t, b, l, ct):
            return t[:, b * 8 + l * 4 + ct:b * 8 + l * 4 + ct + 1]

        def tiles_of(b):
            groups = [[(0, 0), (1, 0), (0, 1)], [(2, 0), (1, 1)], [(3, 0), (2, 1)], [(3, 1)]][b]
            return [(bb, l, ct) for bb, l in groups for ct in range(CT)]

        @block.sync
        def _(sp):
            sp.dma_start(cond_bc, cond.partition_broadcast(P)).then_inc(c_in, 16)
            sp.dma_start(wu[:], wu_dram).then_inc(wu_in, 16)
            for ct in range(CT):
                sp.dma_start(k_sb[:, ct, :], kT[0, ct]).then_inc(k_in[ct], 16)
            sp.dma_start(x_sb[:, 0:CT * T], xT[0]).then_inc(x_in, 16)
            sp.dma_start(wgate[:], gate0).then_inc(wf_in, 16)
            sp.dma_start(wlora_a[:], lora_a).then_inc(wf_in, 16)
            sp.dma_start(wffn[:], w_ffn0).then_inc(wf_in, 16)
            sp.dma_start(wlora_b[:], lora_b).then_inc(wf_in, 16)
            sp.dma_start(wrouter[:], router1).then_inc(wf_in, 16)
            sp.wait_ge(x_in, 16)
            sp.dma_start(x_sb[:, CT * T:2 * CT * T], xT[1]).then_inc(x_in, 16)
            sp.dma_start(stage, wa1).then_inc(raw_in, 16)

            def k_load(b, l, *cts):
                for ct in cts:
                    sp.wait_ge(g_done, s_of(b, l, ct) - 3)
                    sp.dma_start(k_sb[:, ct, :], kT[b, ct]).then_inc(k_in[ct], 16)

            def comb_store(f):
                sp.wait_ge(ct_evac, f + 1)
                sp.dma_start(comb_dram, combT).then_inc(comb_out, 16)
                sp.wait_ge(comb_out, f * 16 + 16)

            def comb_load(f, *experts):
                for e in experts:
                    if e >= 4:
                        sp.wait_ge(hs_done, f * 8 + e - 3)
                    elif f > 0:
                        sp.wait_ge(acc_read, acc_count(f - 1, 1, 0))
                    sp.dma_start(comb[:, e % 4, :], comb_dram[e, :].partition_broadcast(P)).then_inc(comb_in[e % 4], 16)

            def store(f):
                for o in range(CT):
                    sp.wait_ge(acc_read, acc_count(f, 1, o))
                    sp.dma_start(out[f, :, o, :], x_tile(f, o)).then_inc(y_out, 16)

            k_load(1, 0, 0, 1, 2, 3)
            k_load(0, 1, 0, 1)
            sp.wait_ge(wlo_done, 1)
            sp.dma_start(stage, wb1).then_inc(raw_in, 16)
            k_load(0, 1, 2, 3)
            sp.wait_ge(wlo_done, 2)
            for n in (2, 3):
                sp.wait_ge(x_in, 16 * n)
                sp.dma_start(x_sb[:, n * CT * T:(n + 1) * CT * T], xT[n]).then_inc(x_in, 16)
            for b in range(1, B):
                if b + 1 < B:
                    k_load(b + 1, 0, 0, 1, 2, 3)
                else:
                    k_load(b, 1, 0, 1, 2, 3)
                comb_store(b - 1)
                comb_load(b - 1, 0, 1, 2, 3)
                if b + 1 < B:
                    k_load(b, 1, 0, 1)
                    comb_load(b - 1, 4)
                    k_load(b, 1, 2)
                    comb_load(b - 1, 5)
                    k_load(b, 1, 3)
                    comb_load(b - 1, 6, 7)
                else:
                    comb_load(b - 1, 4, 5, 6, 7)
                store(b - 1)
            comb_store(B - 1)
            comb_load(B - 1, *range(NE))
            store(B - 1)
            sp.wait_ge(y_out, 16 * B * CT)

        @block.vector
        def _(dve):
            V = nc.vector

            dve.wait_ge(c_in, 16)
            V.tensor_reduce(tf[:], cond_bc.rearrange("p (b d) -> p b d", b=B), AX.X, ALU.add).then_inc(setup_v, 1)
            V.memset(lntiny[:, 0:1], LN_TINY).then_inc(setup_v, 1)
            V.memset(lntiny[:, 1:2], 0.5 * log(SS_SCALE)).then_inc(setup_v, 1)
            dve.wait_ge(setup_a, 3)
            V.tensor_scalar(half[:], tf[:], 1.0, None, ALU.add).then_inc(setup_v, 1)
            dve.wait_ge(setup_v, 4)
            V.reciprocal(tf[:], half[:]).then_inc(setup_v, 1)
            dve.wait_ge(setup_v, 5)
            V.tensor_scalar(half[:], tf[:], 0.5, 0.5, ALU.mult, ALU.add).then_inc(setup_v, 1)
            V.tensor_scalar(ln_gain[:], tf[:], 0.2, 0.8, ALU.mult, ALU.add).then_inc(setup_v, 1)
            dve.wait_ge(setup_v, 6)
            base = wu[:, 0].rearrange("p l c -> p (l c)")
            for b in range(B):
                V.tensor_scalar(dec[:, b * 8:b * 8 + 8], base, half[:, b:b + 1], None, ALU.mult).then_inc(setup_v, 1)
            dve.wait_ge(setup_v, 11)
            V.tensor_scalar(om[:], dec[:], -1.0, 1.0, ALU.mult, ALU.add).then_inc(setup_v, 1)
            dve.wait_ge(setup_v, 12)
            V.scalar_tensor_tensor(omd2[:], dec[:], 1.0, om[:], ALU.add, ALU.mult).then_inc(decay_done, 1)
            dve.wait_ge(decay_done, 1)

            def cut(tile):
                b, l, ct = tile
                dve.wait_ge(k_in[ct], group(b, l) * 16 + 16)
                if (b, l) != (0, 0):
                    dve.wait_ge(ratio_done, s_of(b, l, ct) - 3)
                V.tensor_scalar(fd[:, ct, :], k_sb[:, ct, :], CLAMP, None, ALU.min).then_inc(kc_done, 1)
                V.tensor_scalar(eu[:, ct, :], k_sb[:, ct, :], wu[:, 1, l, ct:ct + 1], CLAMP, ALU.add, ALU.min).then_inc(kc_done, 1)

            def forward(tile):
                b, l, ct = tile
                d = col(dec, b, l, ct).broadcast_to([P, T])
                dve.wait_ge(ekv_done, s_of(b, l, ct) + 1)
                for f in (fd, fn):
                    V.tensor_tensor_scan(f[:, ct, :], d, f[:, ct, :], 0.0, ALU.mult, ALU.add).then_inc(fwd_done, 1)

            def backward(tile):
                b, l, ct = tile
                s = s_of(b, l, ct)
                d = col(dec, b, l, ct).broadcast_to([P, T - 1])
                for n, f in enumerate((fd, fn)):
                    dve.wait_ge(scaled_done, s * 2 + (n + 1))
                    back = f[:, ct, 0:T - 1][:, ::-1]
                    V.tensor_tensor_scan(back, d, back, f[:, ct, T - 1:T], ALU.mult, ALU.add).then_inc(bwd_done, 1)
                dve.wait_ge(bwd_done, s * 2 + 1)
                dve.wait_ge(exp_done, s * 2 + 2)
                V.tensor_tensor(fd[:, ct, :], fd[:, ct, :], eu[:, ct, :], ALU.add).then_inc(den_done, 1)

            def ratio(tile):
                b, l, ct = tile
                s = s_of(b, l, ct)
                dve.wait_ge(y_done, s + 1)
                dve.wait_ge(num_done, s + 1)
                if l == 1 and b > 0:
                    dve.wait_ge(c1lo_done, b * 4 + ct - 3)
                    dve.wait_ge(logits_done, group(b - 1, 1) + 1)
                dst = cond1[:, ct, :] if l else fn[:, ct, :]
                V.scalar_tensor_tensor(dst, fd[:, ct, :], 1.0 / DEN_MIN, fn[:, ct, :], ALU.min, ALU.mult).then_inc(ratio_done, 1)

            def cut_x(tile):
                b, l, ct = tile
                if l == 0:
                    dve.wait_ge(x_in, b * 16 + 16)
                else:
                    dve.wait_ge(acc_read, acc_count(b, 0, ct))
                s = s_of(b, l, ct)
                if s >= 2:
                    pb, pl = GROUPS[(s - 2) // CT]
                    dve.wait_ge(cond_done[pl], pb * CT + (s - 2) % CT + 1)
                V.tensor_scalar(sig[:, ct % 2, :], x_tile(b, ct), X_MIN, None, ALU.max).then_inc(xc_done, 1)

            def condition1(b, ct):
                s = s_of(b, 1, ct)
                dve.wait_ge(sig_done, s + 1)
                dve.wait_ge(ratio_done, s + 1)
                V.tensor_tensor(cond1[:, ct, :], cond1[:, ct, :], sig[:, ct % 2, :], ALU.mult).then_inc(cond_done[1], 1)

            def top2(b, l):
                z = group(b, l)
                n0 = z * SMALL

                def sync_to(n):
                    dve.wait_ge(small, n0 + n)

                dve.wait_ge(logits_done, z + 1)
                if l == 0:
                    V.tensor_copy(lg[:], lgp[0]).then_inc(small, 1)
                else:
                    dve.wait_ge(lnss_done, b + 1)
                    V.tensor_scalar(rn[:], rn[:], log(NORM_MIN ** 2 * SS_SCALE), None, ALU.max).then_inc(ssmax_done, 1)
                    dve.wait_ge(rn_done, b + 1)
                    V.tensor_tensor(lg[:], lgp[1], rn[:].unsqueeze(2).broadcast_to([P, TT, NE]), ALU.mult).then_inc(small, 1)
                sync_to(1)
                V.memset(mx_ready[:], 0.0)
                for t in range(TT):
                    last = V.max(mx[:, t, :], lg[:, t, :])
                last.then_inc(small, 1)
                sync_to(2)
                V.tensor_tensor(dlt[:], mx[:, :, 1], mx[:, :, 0], ALU.subtract).then_inc(small, 1)
                for t in range(TT):
                    last = V.max_index(mi[:, t, :], mx[:, t, :], lg[:, t, :])
                last.then_inc(small, 1)
                sync_to(4)
                V.tensor_copy(idxf[:], mi[:, :, 0:2]).then_inc(small, 1)
                dve.wait_ge(edl_done, z + 1)
                V.tensor_scalar(den2[:], edl[:], 1.0, None, ALU.add).then_inc(small, 1)
                sync_to(5)
                dve.wait_ge(consts_done, 3 + NE)
                V.tensor_tensor(oh[:], iota[:], idxf[:].unsqueeze(3).broadcast_to([P, TT, 2, NE]), ALU.is_equal).then_inc(small, 1)
                sync_to(6)
                V.reciprocal(rec2[:], den2[:]).then_inc(small, 1)
                sync_to(8)
                gain = ALPHA if l == 0 else 1.0
                V.tensor_scalar(wp[:, :, 0], rec2[:], gain, None, ALU.mult)
                V.scalar_tensor_tensor(wp[:, :, 1], edl[:], gain, rec2[:], ALU.mult, ALU.mult).then_inc(small, 1)
                sync_to(9)
                V.tensor_tensor(oh[:], oh[:], wp[:].unsqueeze(3).broadcast_to([P, TT, 2, NE]), ALU.mult).then_inc(small, 1)
                sync_to(10)
                if l == 0:
                    wide = (oh[:, :, j, :].unsqueeze(3).broadcast_to([P, TT, NE, RANK0]) for j in range(2))
                    V.tensor_tensor(lora_h[:].rearrange("p (t e r) -> p t e r", t=TT, e=NE), *wide, ALU.add).then_inc(cw_done, 1)
                else:
                    V.tensor_tensor(cw[:], oh[:, :, 0, :], oh[:, :, 1, :], ALU.add).then_inc(cw_done, 1)

            def weigh_lora(b):
                dve.wait_ge(lorah_done, b * 4 + 4)
                dve.wait_ge(wrep_evac, b + 1)
                V.tensor_tensor(lora_h[:], hb[:, 0, :], lora_h[:], ALU.mult).then_inc(lorah_used, 1)

            def residual0(b):
                for o in range(CT):
                    dve.wait_ge(ffn0_done, b * 4 + (o + 1))
                    V.tensor_tensor(x_tile(b, o), acc[:, o, :], x_tile(b, o), ALU.add).then_inc(acc_read, 1)

            def weigh(f, e):
                n = f * 8 + e
                dve.wait_ge(h_done, n + 1)
                dve.wait_ge(comb_in[e % 4], f * 32 + e // 4 * 16 + 16)
                if e >= 2:
                    dve.wait_ge(lo_done, n - 1)
                elif f > 0:
                    dve.wait_ge(acc_read, acc_count(f - 1, 1, 0))
                V.tensor_tensor(hs[:, e % 2, :], hb[:, (e + 2) % 3, :], comb[:, e % 4, :], ALU.mult).then_inc(hs_done, 1)

            def residual1(f):
                for o in range(CT):
                    dve.wait_ge(ffn1_done, f * 4 + (o + 1))
                    V.tensor_tensor(x_tile(f, o), acc[:, o, :], x_tile(f, o), ALU.add).then_inc(acc_read, 1)

            def tick(n, b):
                tiles = tiles_of(b)
                if 0 <= n + 1 < len(tiles):
                    cut(tiles[n + 1])
                if 0 <= n < len(tiles):
                    forward(tiles[n])
                if 0 <= n - 1 < len(tiles):
                    cut_x(tiles[n - 1])
                    backward(tiles[n - 1])
                if 0 <= n - 2 < len(tiles):
                    ratio(tiles[n - 2])
                    if tiles[n - 2][1] == 1:
                        condition1(tiles[n - 2][0], tiles[n - 2][2])

            for n in range(-1, 6):
                tick(n, 0)
            top2(0, 0)
            tick(6, 0)
            weigh_lora(0)
            tick(7, 0)
            residual0(0)
            for n in range(8, 12):
                tick(n, 0)
            top2(1, 0)
            tick(12, 0)
            weigh_lora(1)
            tick(13, 0)
            residual0(1)
            top2(0, 1)
            for n in range(-1, 2):
                tick(n, 1)
            weigh(0, 0)
            weigh(0, 1)
            for n in range(2, 8):
                tick(n, 1)
                weigh(0, n)
            tick(8, 1)
            residual1(0)
            tick(9, 1)
            tick(-1, 2)
            tick(0, 2)
            top2(2, 0)
            tick(1, 2)
            top2(1, 1)
            weigh_lora(2)
            tick(2, 2)
            residual0(2)
            weigh(1, 0)
            weigh(1, 1)
            for n in range(2, 8):
                tick(n + 1, 2)
                weigh(1, n)
            tick(9, 2)
            residual1(1)
            tick(-1, 3)
            tick(0, 3)
            top2(3, 0)
            top2(2, 1)
            weigh_lora(3)
            residual0(3)
            weigh(2, 0)
            weigh(2, 1)
            for n in range(1, 6):
                tick(n, 3)
                weigh(2, n + 1)
            weigh(2, 7)
            residual1(2)
            top2(3, 1)
            for e in range(NE):
                weigh(3, e)
            residual1(3)

        @block.scalar
        def _(act):
            A = nc.scalar.activation
            nc.scalar.preload_act_table_set("natural_log_exp_and_others")
            act.wait_ge(wu_in, 16)
            A(wu[:, 0], wu[:, 0], ACT.Exp).then_inc(setup_a, 1)
            act.wait_ge(setup_a, 1)
            A(wu[:, 0], wu[:, 0], ACT.Exp, scale=-1.0).then_inc(setup_a, 1)
            act.wait_ge(setup_v, 1)
            A(tf[:], tf[:], ACT.Exp, scale=-1.0).then_inc(setup_a, 1)

            def exps(tile):
                b, l, ct = tile
                for n, buf in enumerate((fd, eu)):
                    act.wait_ge(kc_done, s_of(b, l, ct) * 2 + (n + 1))
                    A(buf[:, ct, :], buf[:, ct, :], ACT.Exp).then_inc(exp_done, 1)

            def scale(tile):
                b, l, ct = tile
                for n, f in enumerate((fd, fn)):
                    act.wait_ge(fwd_done, s_of(b, l, ct) * 2 + (n + 1))
                    A(f[:, ct, 0:T - 1], f[:, ct, 0:T - 1], ACT.Copy, scale=col(omd2, b, l, ct)).then_inc(scaled_done, 1)

            def log_den(tile):
                b, l, ct = tile
                act.wait_ge(den_done, s_of(b, l, ct) + 1)
                A(fd[:, ct, :], fd[:, ct, :], ACT.Ln, bias=lntiny[:, 0:1]).then_inc(lnd_done, 1)

            def inverse_den(tile):
                b, l, ct = tile
                act.wait_ge(lnd_done, s_of(b, l, ct) + 1)
                A(fd[:, ct, :], fd[:, ct, :], ACT.Exp, scale=-1.0).then_inc(y_done, 1)

            def sigmoid(tile, step):
                b, l, ct = tile
                s, buf = s_of(b, l, ct), sig[:, ct % 2, :]
                if step == 0:
                    act.wait_ge(xc_done, s + 1)
                    A(buf, buf, ACT.Exp, scale=-1.0).then_inc(sig_exp, 1)
                elif step == 1:
                    act.wait_ge(sig_exp, s + 1)
                    A(buf, buf, ACT.Ln, bias=1.0).then_inc(sig_ln, 1)
                else:
                    act.wait_ge(sig_ln, s + 1)
                    A(buf, buf, ACT.Exp, scale=-1.0, bias=ln_gain[:, b:b + 1]).then_inc(sig_done, 1)

            def tick(n, b):
                tiles = tiles_of(b)
                if 0 <= n + 1 < len(tiles):
                    exps(tiles[n + 1])
                with_sig = 0 <= n - 1 < len(tiles)
                if with_sig:
                    sigmoid(tiles[n - 1], 0)
                if 0 <= n < len(tiles):
                    scale(tiles[n])
                if with_sig:
                    sigmoid(tiles[n - 1], 1)
                if 0 <= n - 1 < len(tiles):
                    log_den(tiles[n - 1])
                if with_sig:
                    sigmoid(tiles[n - 1], 2)
                if 0 <= n - 1 < len(tiles):
                    inverse_den(tiles[n - 1])

            def edl_step(b, l):
                act.wait_ge(small, group(b, l) * SMALL + 3)
                A(edl[:], dlt[:], ACT.Exp).then_inc(edl_done, 1)

            def split_hi(f, ct):
                if f > 0:
                    act.wait_ge(h_done, f * 8)
                act.wait_ge(cond_done[1], f * 4 + ct + 1)
                A(cond1_hi[:, ct, :], cond1[:, ct, :], ACT.Copy).then_inc(c1hi_done, 1)

            def hi_part(f, e):
                n = f * 8 + e
                act.wait_ge(hs_done, n + 1)
                if e >= 2:
                    act.wait_ge(exp_out_done, f * 7 + e - 1)
                elif f > 0:
                    act.wait_ge(acc_read, acc_count(f - 1, 1, 0))
                A(hs_hi[:, e % 2, :], hs[:, e % 2, :], ACT.Copy).then_inc(hi_done, 1)

            def gates1(b):
                act.wait_ge(logits_done, group(b, 1) + 1)
                A(rn[:], ssp, ACT.Ln, scale=SS_SCALE, bias=lntiny[:, 0:1]).then_inc(lnss_done, 1)
                act.wait_ge(ssmax_done, b + 1)
                A(rn[:], rn[:], ACT.Exp, scale=-0.5, bias=lntiny[:, 1:2]).then_inc(rn_done, 1)
                edl_step(b, 1)

            def evac_combT(f):
                act.wait_ge(ct_done, f + 1)
                A(combT, hb[0:NE, 1, :], ACT.Copy).then_inc(ct_evac, 1)

            def weights_hi(which, c):
                act.wait_ge(raw_in, 16 * (which + 1))
                hi = (wa_hi[:].rearrange("p e k r -> p (e k r)"), wb_hi[:].rearrange("p e o -> p (e o)"))[which]
                A(hi[:, c * 1024:(c + 1) * 1024], stage[:, c * 1024:(c + 1) * 1024], ACT.Copy).then_inc(whi_done, 1)

            act.wait_ge(setup_v, 7)
            A(ln_gain[:], ln_gain[:], ACT.Ln).then_inc(setup_a, 1)
            act.wait_ge(setup_a, 4)
            act.wait_ge(decay_done, 1)

            def wrep_to_sbuf(b):
                act.wait_ge(wrep_done, b + 1)
                A(lora_h[:], hb[:, 1, :], ACT.Copy).then_inc(wrep_evac, 1)

            for n in range(-1, 6):
                tick(n, 0)
                if n >= 2:
                    weights_hi(0, n - 2)
            edl_step(0, 0)
            tick(6, 0)
            wrep_to_sbuf(0)
            tick(7, 0)
            for n in range(8, 12):
                tick(n, 0)
                weights_hi(1, n - 8)
            edl_step(1, 0)
            tick(12, 0)
            wrep_to_sbuf(1)
            tick(13, 0)
            for ct in range(CT):
                split_hi(0, ct)
            gates1(0)
            tick(-1, 1)
            evac_combT(0)
            tick(0, 1)
            tick(1, 1)
            hi_part(0, 0)
            hi_part(0, 1)
            for n in range(2, 8):
                tick(n, 1)
                hi_part(0, n)
            tick(8, 1)
            tick(9, 1)
            tick(-1, 2)
            for ct in range(CT):
                split_hi(1, ct)
            tick(0, 2)
            edl_step(2, 0)
            tick(1, 2)
            gates1(1)
            wrep_to_sbuf(2)
            tick(2, 2)
            evac_combT(1)
            hi_part(1, 0)
            hi_part(1, 1)
            for n in range(2, 8):
                tick(n + 1, 2)
                hi_part(1, n)
            tick(9, 2)
            tick(-1, 3)
            for ct in range(CT):
                split_hi(2, ct)
            tick(0, 3)
            edl_step(3, 0)
            gates1(2)
            wrep_to_sbuf(3)
            evac_combT(2)
            hi_part(2, 0)
            hi_part(2, 1)
            for n in range(1, 6):
                tick(n, 3)
                hi_part(2, n + 1)
            hi_part(2, 7)
            for ct in range(CT):
                split_hi(3, ct)
            gates1(3)
            evac_combT(3)
            for e in range(NE):
                hi_part(3, e)

        @block.gpsimd
        def _(pool):
            G = nc.gpsimd
            G.memset(ident[:], 0.0).then_inc(consts_done, 1)
            pool.wait_ge(consts_done, 1)
            G.affine_select(out=ident[:], in_=ident[:], compare_op=ALU.not_equal, fill=1.0, base=0,
                            pattern=[[-1, P]], channel_multiplier=1).then_inc(consts_done, 1)
            G.memset(ones[:], 1.0).then_inc(consts_done, 1)
            for e in range(NE):
                G.memset(iota[:, :, :, e:e + 1], float(e)).then_inc(consts_done, 1)

            def ekv_step(tile):
                b, l, ct = tile
                s = s_of(b, l, ct)
                if s >= CT:
                    pb, pl = GROUPS[s // CT - 1]
                    pool.wait_ge(cond_done[pl], pb * CT + ct + 1)
                pool.wait_ge(exp_done, s * 2 + 1)
                G.tensor_tensor(fn[:, ct, :], fd[:, ct, :], k_sb[:, ct, :], ALU.mult).then_inc(ekv_done, 1)

            def numerator(tile):
                b, l, ct = tile
                s = s_of(b, l, ct)
                pool.wait_ge(den_done, s + 1)
                G.tensor_tensor(eu[:, ct, :], eu[:, ct, :], k_sb[:, ct, :], ALU.mult).then_inc(g_done, 1)
                pool.wait_ge(g_done, s + 1)
                pool.wait_ge(bwd_done, s * 2 + 2)
                G.tensor_tensor(fn[:, ct, :], fn[:, ct, :], eu[:, ct, :], ALU.add).then_inc(num_done, 1)

            def condition0(b, ct):
                s = s_of(b, 0, ct)
                pool.wait_ge(sig_done, s + 1)
                pool.wait_ge(ratio_done, s + 1)
                if b > 0:
                    pool.wait_ge(cond0_used, b * 4 + ct - 3)
                G.tensor_tensor(cond0[:, ct, :], fn[:, ct, :], sig[:, ct % 2, :], ALU.mult).then_inc(cond_done[0], 1)

            def tick(n, b):
                tiles = tiles_of(b)
                if 0 <= n + 1 < len(tiles):
                    ekv_step(tiles[n + 1])
                if 0 <= n - 1 < len(tiles):
                    numerator(tiles[n - 1])
                if 0 <= n - 2 < len(tiles) and tiles[n - 2][1] == 0:
                    condition0(tiles[n - 2][0], tiles[n - 2][2])

            def split_lo(f, ct):
                pool.wait_ge(c1hi_done, f * 4 + (ct + 1))
                G.tensor_tensor(cond1_lo[:, ct, :], cond1[:, ct, :], cond1_hi[:, ct, :].bitcast(F32), ALU.subtract).then_inc(c1lo_done, 1)

            def lo_part(f, e):
                n = f * 8 + e
                pool.wait_ge(hi_done, n + 1)
                G.tensor_tensor(hs_lo[:, e % 2, :], hs[:, e % 2, :], hs_hi[:, e % 2, :].bitcast(F32), ALU.subtract).then_inc(lo_done, 1)

            def squares(b, ct):
                pool.wait_ge(cond_done[1], b * 4 + ct + 1)
                n0 = b * 6
                if ct == 0:
                    if b > 0:
                        pool.wait_ge(comb_out, b * 16)
                    G.tensor_tensor(ss[:], cond1[:, 0, :], cond1[:, 0, :], ALU.mult).then_inc(sq_steps, 1)
                    return
                if ct > 1:
                    pool.wait_ge(sq_steps, n0 + (2 * ct - 1))
                G.tensor_tensor(sq[:], cond1[:, ct, :], cond1[:, ct, :], ALU.mult).then_inc(sq_steps, 1)
                pool.wait_ge(sq_steps, n0 + 2 * ct)
                G.tensor_tensor(ss[:], ss[:], sq[:], ALU.add).then_inc(ss_done if ct == CT - 1 else sq_steps, 1)

            def weights_lo(which, c):
                pool.wait_ge(whi_done, which * 4 + c + 1)
                hi, lo = ((wa_hi, wa_lo), (wb_hi, wb_lo))[which]
                how = ("p e k r -> p (e k r)", "p e o -> p (e o)")[which]
                part = slice(c * 1024, (c + 1) * 1024)
                last = G.tensor_tensor(lo[:].rearrange(how)[:, part], stage[:, part],
                                       hi[:].rearrange(how)[:, part].bitcast(F32), ALU.subtract)
                if c == 3:
                    last.then_inc(wlo_done, 1)

            for n in range(-1, 12):
                tick(n, 0)
                if 2 <= n < 6:
                    weights_lo(0, n - 2)
                if n >= 8:
                    weights_lo(1, n - 8)
                if n >= 10:
                    squares(0, n - 10)
            for n in (12, 13):
                tick(n, 0)
                squares(0, n - 10)
            for ct in range(CT):
                split_lo(0, ct)
            for n in range(-1, 2):
                tick(n, 1)
            lo_part(0, 0)
            lo_part(0, 1)
            for n in range(2, 8):
                tick(n, 1)
                if n >= 6:
                    squares(1, n - 6)
                lo_part(0, n)
            for n in (8, 9):
                tick(n, 1)
                squares(1, n - 6)
            for n in (-1, 0):
                tick(n, 2)
                split_lo(1, 2 * n + 2)
                split_lo(1, 2 * n + 3)
            tick(1, 2)
            tick(2, 2)
            lo_part(1, 0)
            lo_part(1, 1)
            for n in range(2, 8):
                tick(n + 1, 2)
                if n >= 5:
                    squares(2, n - 5)
                lo_part(1, n)
            tick(9, 2)
            squares(2, 3)
            for n in (-1, 0):
                tick(n, 3)
                split_lo(2, 2 * n + 2)
                split_lo(2, 2 * n + 3)
            lo_part(2, 0)
            lo_part(2, 1)
            for n in range(1, 6):
                tick(n, 3)
                if n >= 2:
                    squares(3, n - 2)
                lo_part(2, n + 1)
            lo_part(2, 7)
            for ct in range(CT):
                split_lo(3, ct)
            for e in range(NE):
                lo_part(3, e)

        @block.tensor
        def _(pe):
            MM = nc.tensor.matmul
            pe.wait_ge(wf_in, 16 * 5)
            pe.wait_ge(consts_done, 3 + NE)

            def router1_step(b):
                if b + 1 < B:
                    pe.wait_ge(small, group(b + 1, 0) * SMALL + 1)
                pe.wait_ge(cond_done[1], b * 4 + 4)
                for t in range(TT):
                    for k in range(CT):
                        MM(lgp[1][:, t, :], cond1[:, k, t * P:(t + 1) * P], wrouter[:, k, :], start=k == 0, stop=k == CT - 1)
                pe.wait_ge(ss_done, b + 1)
                for t in range(TT):
                    mm = MM(ssp[:, t:t + 1], ss[:, t * P:(t + 1) * P], ones[:, 0:1], start=True, stop=True)
                mm.then_inc(logits_done, 1)

            def lora_in(b, k):
                MM(hb[:, 0, :], wlora_a[:, k, :], cond0[:, k, :], start=k == 0, stop=k == CT - 1).then_inc(lorah_done, 1)

            def gate0_logits(b, t, k, start):
                mm = MM(lgp[0][:, t, :], cond0[:, k, t * P:(t + 1) * P], wgate[:, k, :], start=start, stop=k == CT - 1,
                        skip_group_check=True)
                if t == TT - 1 and k == CT - 1:
                    mm.then_inc(logits_done, 1)

            def ffn0_tile(b, k, gates):
                for o in range(CT):
                    gates(o)
                    if k == 0 and b > 0:
                        pe.wait_ge(acc_read, acc_before(b, 0, o))
                    mm = MM(acc[:, o, :], wffn[:, k, o * P:(o + 1) * P], cond0[:, k, :], start=k == 0, stop=False)
                mm.then_inc(cond0_used, 1)

            def ffn0_arriving(b):
                for k in range(CT):
                    pe.wait_ge(cond_done[0], b * 4 + k + 1)
                    lora_in(b, k)
                    ffn0_tile(b, k, lambda t: gate0_logits(b, t, k, k == 0 and t == 0))

            def ffn0_gates_first(b):
                pe.wait_ge(cond_done[0], b * 4 + 4)
                for k in range(CT):
                    lora_in(b, k)

                def gates(t):
                    for k in range(CT):
                        gate0_logits(b, t, k, k == 0)

                ffn0_tile(b, 0, gates)

            def lora_weights(b):
                pe.wait_ge(cw_done, group(b, 0) + 1)
                for t in range(TT):
                    mm = MM(hb[:, 1, t * P:(t + 1) * P], lora_h[:, t * P:(t + 1) * P], ident[:], start=True, stop=True)
                mm.then_inc(wrep_done, 1)

            def lora_out(b):
                pe.wait_ge(lorah_used, b + 1)
                for o in range(CT):
                    MM(acc[:, o, :], wlora_b[:, o * P:(o + 1) * P], lora_h[:], start=False, stop=True).then_inc(ffn0_done, 1)

            def turn_comb(f):
                pe.wait_ge(cw_done, group(f, 1) + 1)
                if f + 1 < B:
                    pe.wait_ge(wrep_evac, f + 2)
                for t in range(TT):
                    mm = MM(hb[0:NE, 1, t * P:(t + 1) * P], cw[:, t, :], ident[:], start=True, stop=True)
                mm.then_inc(ct_done, 1)

            def hidden(f, e):
                if e == 2:
                    pe.wait_ge(ct_evac, f + 1)
                n = 0
                for k in range(CT):
                    for w, c in ((wa_hi, cond1_hi), (wa_hi, cond1_lo), (wa_lo, cond1_hi)):
                        mm = MM(hb[:, (e + 2) % 3, :], w[:, e, k, :], c[:, k, :], start=n == 0, stop=n == 3 * CT - 1)
                        n += 1
                mm.then_inc(h_done, 1)

            def expert_out(f, e):
                pe.wait_ge(lo_done, f * 8 + (e + 1))
                for o in range(CT):
                    if e == 0:
                        pe.wait_ge(acc_read, acc_before(f, 1, o))
                    for n, (w, h) in enumerate(((wb_hi, hs_hi), (wb_hi, hs_lo), (wb_lo, hs_hi))):
                        mm = MM(acc[:, o, :], w[:, e, o * P:(o + 1) * P], h[:, e % 2, :], start=e == 0 and n == 0,
                                stop=e == NE - 1 and n == 2)
                    if e == NE - 1:
                        mm.then_inc(ffn1_done, 1)
                if e < NE - 1:
                    mm.then_inc(exp_out_done, 1)

            def ffn1_first(f):
                pe.wait_ge(c1lo_done, f * 4 + 4)
                pe.wait_ge(wlo_done, 2)
                hidden(f, 0)

            def ffn1_rest(f):
                hidden(f, 1)
                for e in range(NE):
                    if e + 2 < NE:
                        hidden(f, e + 2)
                    expert_out(f, e)

            def no_gates(t):
                pass

            for b in (0, 1):
                ffn0_arriving(b)
                lora_weights(b)
                lora_out(b)
            router1_step(0)
            ffn1_first(0)
            turn_comb(0)
            ffn1_rest(0)
            for b in (2, 3):
                ffn0_gates_first(b)
                ffn0_tile(b, 1, no_gates)
                router1_step(b - 1)
                ffn0_tile(b, 2, no_gates)
                lora_weights(b)
                ffn0_tile(b, 3, no_gates)
                turn_comb(b - 1)
                lora_out(b)
                ffn1_first(b - 1)
                ffn1_rest(b - 1)
            router1_step(3)
            ffn1_first(3)
            turn_comb(3)
            ffn1_rest(3)


_SHAPES = {
    "xT": (B, P, CT, T), "kT": (B, CT, P, T), "cond": (1, B * P), "wu": (P, 2, 2, CT), "w_ffn0": (P, CT, C),
    "gate0": (P, CT, NE), "lora_a": (P, CT, P), "lora_b": (P, C), "router1": (P, CT, NE),
    "wa1": (P, NE * CT * P), "wb1": (P, NE * C),
}


def kernel(x, fside_BxSxS_0, cond_512, L0_cond_w, L0_cond_u, L0_ffn_W, L0_ffn_gate_w, L0_ffn_A, L0_ffn_B,
           L1_cond_w, L1_cond_u, L1_ffn_router_w, L1_ffn_Wa, L1_ffn_Wb):
    import numpy as np
    import concourse.bacc as bacc
    from concourse.bass_utils import run_bass_kernel_spmd

    def rows(w):
        return np.asarray(w).reshape(CT, P, -1).transpose(1, 0, 2)

    x, k = np.asarray(x), np.asarray(fside_BxSxS_0)
    wu = np.stack([np.asarray(a).reshape(CT, P) for a in (L0_cond_w, L1_cond_w, L0_cond_u, L1_cond_u)])
    data = {
        "xT": x.reshape(B, T, CT, P).transpose(0, 3, 2, 1),
        "kT": k.reshape(B, T, CT, P).transpose(0, 2, 3, 1),
        "cond": np.asarray(cond_512).reshape(1, B * P),
        "wu": wu.reshape(2, 2, CT, P).transpose(3, 0, 1, 2),
        "w_ffn0": rows(np.asarray(L0_ffn_W).T),
        "gate0": rows(np.asarray(L0_ffn_gate_w).T),
        "lora_a": rows(np.asarray(L0_ffn_A).reshape(P, C).T),
        "lora_b": np.asarray(L0_ffn_B).transpose(0, 2, 1).reshape(P, C),
        "router1": rows(L1_ffn_router_w),
        "wa1": np.asarray(L1_ffn_Wa).reshape(NE, CT, P, P).transpose(2, 0, 1, 3).reshape(P, -1),
        "wb1": np.asarray(L1_ffn_Wb).transpose(1, 0, 2).reshape(P, -1),
    }
    nc = bacc.Bacc("TRN2", target_bir_lowering=False, num_devices=1)
    arrays, args = {}, []
    for name, shape in _SHAPES.items():
        arrays[name + "_dram"] = np.ascontiguousarray(data[name])
        args.append(nc.dram_tensor(name + "_dram", shape, F32, kind="ExternalInput").ap())
    out = nc.dram_tensor("out_dram", (B, P, CT, T), F32, kind="ExternalOutput").ap()
    scratch = nc.dram_tensor("comb_dram", (NE, T), F32).ap()
    build(nc, *args, out, scratch)
    r = run_bass_kernel_spmd(nc, [arrays], core_ids=[0])
    got = np.asarray(r.results[0]["out_dram"])
    return np.ascontiguousarray(got.transpose(0, 3, 2, 1)).reshape(B, T, C)
```

```python
from contextlib import ExitStack
from math import log

import concourse.bass as bass
from concourse import mybir

F32 = mybir.dt.float32
F32R = mybir.dt.float32r
U32 = mybir.dt.uint32
ALU = mybir.AluOpType
ACT = mybir.ActivationFunctionType
AX = mybir.AxisListType

P = 128
B, T, C = 4, 512, 512
CT = C // P
TT = T // P
NE = 8
RANK0 = 16
ALPHA = 16.0
CLAMP = 30.0
DEN_MIN = 1e-8
X_MIN = -43.0
LN_TINY = 2.0 ** -63
NORM_MIN = 1e-12
SS_SCALE = 2.0 ** 20
SMALL = 10


def build(nc, xT, kT, cond, wu_dram, w_ffn0, gate0, lora_a, lora_b, router1, wa1, wb1, out,
          comb_dram):
    with ExitStack() as ctx:
        def sb(name, shape, dt=F32):
            return ctx.enter_context(nc.sbuf_tensor(name, shape, dt))

        def sem(name):
            return ctx.enter_context(nc.semaphore(name))

        x_sb = sb("x_sb", [P, B * CT * T])
        k_sb = sb("k_sb", [P, CT, T])
        cond0 = sb("cond0", [P, CT, T])
        cond1 = sb("cond1", [P, CT, T])
        cond1_hi = sb("cond1_hi", [P, CT, T], F32R)
        cond1_lo = sb("cond1_lo", [P, CT, T], F32R)
        wffn = sb("wffn", [P, CT, C])
        wgate = sb("wgate", [P, CT, NE])
        wrouter = sb("wrouter", [P, CT, NE])
        wlora_a = sb("wlora_a", [P, CT, P])
        wlora_b = sb("wlora_b", [P, C])
        wa_hi = sb("wa_hi", [P, NE, CT, P], F32R)
        wa_lo = sb("wa_lo", [P, NE, CT, P], F32R)
        wb_hi = sb("wb_hi", [P, NE, C], F32R)
        wb_lo = sb("wb_lo", [P, NE, C], F32R)
        eu = sb("eu", [P, CT, T])
        fd = sb("fd", [P, CT, T])
        fn = sb("fn", [P, CT, T])
        sig = sb("sig", [P, 2, T])
        lora_h = sb("lora_h", [P, T])
        sq = sb("sq", [P, T])
        ss = sb("ss", [P, T])
        combT = ss[0:NE, :]
        comb = sb("comb", [P, 4, T])
        hs = sb("hs", [P, 2, T])
        hs_hi = sb("hs_hi", [P, 2, T], F32R)
        hs_lo = sb("hs_lo", [P, 2, T], F32R)
        ident = sb("ident", [P, P])
        ones = sb("ones", [P, 2])
        iota = sb("iota", [P, TT, 2, NE])
        wu = sb("wu", [P, 2, 2, CT])
        dec = sb("dec", [P, B * 2 * CT])
        omd2 = sb("omd2", [P, B * 2 * CT])
        om = sb("om", [P, B * 2 * CT])
        tf = sb("tf", [P, B])
        half = sb("half", [P, B])
        ln_gain = sb("ln_gain", [P, B])
        lntiny = sb("lntiny", [P, 2])
        lg = sb("lg", [P, TT, NE])
        mx = sb("mx", [P, TT, 8])
        mi = sb("mi", [P, TT, 8], U32)
        idxf = sb("idxf", [P, TT, 2])
        oh = sb("oh", [P, TT, 2, NE])
        dlt = sb("dlt", [P, TT])
        edl = sb("edl", [P, TT])
        den2 = sb("den2", [P, TT])
        rec2 = sb("rec2", [P, TT])
        wp = sb("wp", [P, TT, 2])
        cw = sb("cw", [P, TT, NE])
        rn = sb("rn", [P, TT])

        acc = ctx.enter_context(nc.psum_tensor("acc", [P, 4, T], F32))
        hb = ctx.enter_context(nc.psum_tensor("hb", [P, 3, T], F32))
        mis = ctx.enter_context(nc.psum_tensor("mis", [P, T], F32))
        lgp = [mis[:, 0:32].rearrange("p (t e) -> p t e", t=TT), mis[:, 32:64].rearrange("p (t e) -> p t e", t=TT)]
        ssp = mis[:, 64:64 + TT]
        HALF, QUARTER = NE * C // 2, NE * C // 4
        stage = {(w, h): x_sb[:, i * HALF:(i + 1) * HALF] for w, h, i in ((0, 0, 1), (1, 0, 2), (0, 1, 3), (1, 1, 2))}
        QUARTERS = [(0, 0), (0, 1), (1, 0), (1, 1), (0, 2), (0, 3), (1, 2), (1, 3)]
        cond_bc = comb[:, 0, :]

        x_in, c_in, wu_in, wf_in = sem("x_in"), sem("c_in"), sem("wu_in"), sem("wf_in")
        raw_in = {(w, h): sem(f"raw_in{w}{h}") for w in range(2) for h in range(2)}
        k_in = [sem(f"k_in{i}") for i in range(CT)]
        comb_in = [sem(f"comb_in{i}") for i in range(4)]
        comb_spread, comb_copied = sem("comb_spread"), sem("comb_copied")
        comb_out, y_out = sem("comb_out"), sem("y_out")
        consts_done, setup_v, setup_a, decay_done = (sem(n) for n in ("consts_done", "setup_v", "setup_a", "decay_done"))
        kc_done, fwd_done, bwd_done, den_done, ratio_done = (sem(n) for n in ("kc_done", "fwd_done", "bwd_done", "den_done", "ratio_done"))
        exp_done, scaled_done, lnd_done, y_done = (sem(n) for n in ("exp_done", "scaled_done", "lnd_done", "y_done"))
        ekv_done, g_done, num_done = sem("ekv_done"), sem("g_done"), sem("num_done")
        xc_done, sig_exp, sig_ln, sig_done = (sem(n) for n in ("xc_done", "sig_exp", "sig_ln", "sig_done"))
        cond_done = [sem("cond0_done"), sem("cond1_done")]
        squared, sq_added = sem("squared"), sem("sq_added")
        logits_done, small, edl_done, cw_done = sem("logits_done"), sem("small"), sem("edl_done"), sem("cw_done")
        lnss_done, ssmax_done, rn_done = sem("lnss_done"), sem("ssmax_done"), sem("rn_done")
        lorah_done, cond0_used, wrep_done, wrep_evac, lorah_used = sem("lorah_done"), sem("cond0_used"), sem("wrep_done"), sem("wrep_evac"), sem("lorah_used")
        ffn0_done, acc_read, ct_done, ct_evac = sem("ffn0_done"), sem("acc_read"), sem("ct_done"), sem("ct_evac")
        h_done, hs_done, hi_done, lo_done, exp_out_done = (sem(n) for n in ("h_done", "hs_done", "hi_done", "lo_done", "exp_out_done"))
        ffn1_done = sem("ffn1_done")
        c1hi_done, c1lo_done = sem("c1hi_done"), sem("c1lo_done")
        whi_done = sem("whi_done")
        wlo_done = [sem("wlo_pool_done"), sem("wlo_dve_done")]

        block = ctx.enter_context(nc.Block())

        GROUPS = [(0, 0), (0, 1), (1, 0), (2, 0), (1, 1), (3, 0), (2, 1), (3, 1)]
        WKV = [(0, 0), (0, 1), (1, 0), (1, 1), (2, 0), (3, 0), (2, 1), (3, 1)]
        APART = [(0, 1), (1, 1)]
        RUNS = [WKV[0:5], WKV[5:7], WKV[7:8]]

        def group(b, l):
            return GROUPS.index((b, l))

        def s_of(b, l, ct):
            return WKV.index((b, l)) * CT + ct

        def sig_of(b, l, ct):
            return group(b, l) * CT + ct

        def k_count(b, l):
            return 16 * max(1, WKV.index((b, l)))

        def acc_count(b, l, o):
            return group(b, l) * CT + o + 1

        def acc_before(b, l, o):
            return acc_count(b, l, o) - CT

        def x_tile(b, ct):
            return x_sb[:, (b * CT + ct) * T:(b * CT + ct + 1) * T]

        def col(t, b, l, ct):
            return t[:, b * 8 + l * 4 + ct:b * 8 + l * 4 + ct + 1]

        SPREAD = 2
        COMB_LOADS = [(f, e) for f in range(B) for e in range(NE) if f > 0 or e >= SPREAD]

        def comb_count(f, e):
            return 16 * sum(n % 4 == e % 4 for _, n in COMB_LOADS[:COMB_LOADS.index((f, e)) + 1])

        TILES = [[(b, l, ct) for b, l in run for ct in range(CT)] for run in RUNS]

        def tile_at(run, n):
            return TILES[run][n] if 0 <= n < len(TILES[run]) else None

        def ekuv(b, l, ct):
            return (cond1 if (b, l) == (0, 0) else k_sb)[:, ct, :]

        def sigma(b, l, ct):
            return hs[:, ct - 2, :] if (b, l) in APART and ct >= 2 else sig[:, ct % 2, :]

        def sig_apart(tile):
            return tile[:2] in APART

        def weights_lo(engine, E, n):
            which, c = QUARTERS[n]
            engine.wait_ge(whi_done, n + 1)
            hi, lo = ((wa_hi, wa_lo), (wb_hi, wb_lo))[which]
            how = ("p e k r -> p (e k r)", "p e o -> p (e o)")[which]
            part = slice(c * QUARTER, (c + 1) * QUARTER)
            raw = stage[which, c // 2][:, c % 2 * QUARTER:(c % 2 + 1) * QUARTER]
            E.tensor_tensor(lo[:].rearrange(how)[:, part], raw,
                            hi[:].rearrange(how)[:, part].bitcast(F32), ALU.subtract).then_inc(wlo_done[n // 4], 1)

        def add_square(engine, E, b, ct):
            engine.wait_ge(squared, b * 4 + ct + 1)
            if ct > 1:
                engine.wait_ge(sq_added, b * 3 + (ct - 1))
            E.tensor_tensor(ss[:], ss[:], sq[:], ALU.add).then_inc(sq_added, 1)

        @block.sync
        def _(sp):
            sp.dma_start(cond_bc, cond.partition_broadcast(P)).then_inc(c_in, 16)
            sp.dma_start(wu[:], wu_dram).then_inc(wu_in, 16)
            for ct in range(CT):
                sp.dma_start(k_sb[:, ct, :], kT[0, ct]).then_inc(k_in[ct], 16)
            sp.dma_start(x_sb[:, 0:CT * T], xT[0]).then_inc(x_in, 16)
            sp.dma_start(wgate[:], gate0).then_inc(wf_in, 16)
            sp.dma_start(wlora_a[:], lora_a).then_inc(wf_in, 16)
            sp.dma_start(wffn[:], w_ffn0).then_inc(wf_in, 16)
            sp.dma_start(wlora_b[:], lora_b).then_inc(wf_in, 16)
            sp.dma_start(wrouter[:], router1).then_inc(wf_in, 16)
            sp.dma_start(stage[0, 0], wa1[:, 0:HALF]).then_inc(raw_in[0, 0], 16)
            sp.dma_start(stage[1, 0], wb1[:, 0:HALF]).then_inc(raw_in[1, 0], 16)
            sp.dma_start(stage[0, 1], wa1[:, HALF:]).then_inc(raw_in[0, 1], 16)

            def x_load(b):
                sp.wait_ge(x_in, 16 * b)
                sp.dma_start(x_sb[:, b * CT * T:(b + 1) * CT * T], xT[b]).then_inc(x_in, 16)

            def k_load(b, l, *cts):
                for ct in cts:
                    sp.wait_ge(num_done, s_of(b, l, ct) - 3)
                    sp.dma_start(k_sb[:, ct, :], kT[b, ct]).then_inc(k_in[ct], 16)

            def comb_store(f):
                sp.wait_ge(ct_evac, f + 1)
                sp.dma_start(comb_dram[f % 2], combT).then_inc(comb_out, 16)
                sp.wait_ge(comb_out, f * 16 + 16)

            def comb_load(f, *experts):
                for e in experts:
                    if f > 0 or e >= 4:
                        sp.wait_ge(hs_done, f * 8 + e - 3)
                    sp.dma_start(comb[:, e % 4, :], comb_dram[f % 2, e, :].partition_broadcast(P)).then_inc(comb_in[e % 4], 16)

            def store(f):
                for o in range(CT):
                    sp.wait_ge(acc_read, acc_count(f, 1, o))
                    sp.dma_start(out[f, :, o, :], x_tile(f, o)).then_inc(y_out, 16)

            k_load(1, 0, 0, 1)
            sp.wait_ge(wlo_done[0], 2)
            x_load(1)
            k_load(1, 0, 2, 3)
            sp.wait_ge(wlo_done[0], 4)
            sp.dma_start(stage[1, 1], wb1[:, HALF:]).then_inc(raw_in[1, 1], 16)
            comb_store(0)
            comb_load(0, 2, 3)
            for n in range(CT):
                comb_load(0, 4 + n)
                k_load(1, 1, n)
            k_load(2, 0, 0)
            sp.wait_ge(wlo_done[1], 4)
            x_load(2)
            k_load(2, 0, 1, 2, 3)
            x_load(3)
            store(0)
            k_load(3, 0, 0, 1, 2, 3)
            comb_store(1)
            comb_load(1, 0, 1, 2, 3)
            k_load(2, 1, 0)
            comb_load(1, 4)
            k_load(2, 1, 1)
            comb_load(1, 5, 6)
            k_load(2, 1, 2)
            comb_load(1, 7)
            k_load(2, 1, 3)
            store(1)
            k_load(3, 1, 0, 1, 2, 3)
            comb_store(2)
            comb_load(2, *range(NE))
            comb_store(3)
            comb_load(3, 0, 1, 2, 3)
            store(2)
            comb_load(3, 4, 5, 6, 7)
            store(3)
            sp.wait_ge(y_out, 16 * B * CT)

        @block.vector
        def _(dve):
            V = nc.vector

            def decays():
                dve.wait_ge(c_in, 16)
                V.tensor_reduce(tf[:], cond_bc.rearrange("p (b d) -> p b d", b=B), AX.X, ALU.add).then_inc(setup_v, 1)
                V.memset(lntiny[:, 0:1], LN_TINY).then_inc(setup_v, 1)
                V.memset(lntiny[:, 1:2], 0.5 * log(SS_SCALE)).then_inc(setup_v, 1)
                dve.wait_ge(setup_a, 3)
                V.tensor_scalar(half[:], tf[:], 1.0, None, ALU.add).then_inc(setup_v, 1)
                dve.wait_ge(setup_v, 4)
                V.reciprocal(tf[:], half[:]).then_inc(setup_v, 1)
                dve.wait_ge(setup_v, 5)
                V.tensor_scalar(half[:], tf[:], 0.5, 0.5, ALU.mult, ALU.add).then_inc(setup_v, 1)
                V.tensor_scalar(ln_gain[:], tf[:], 0.2, 0.8, ALU.mult, ALU.add).then_inc(setup_v, 1)
                dve.wait_ge(setup_v, 6)
                base = wu[:, 0].rearrange("p l c -> p (l c)")
                for b in range(B):
                    V.tensor_scalar(dec[:, b * 8:b * 8 + 8], base, half[:, b:b + 1], None, ALU.mult).then_inc(setup_v, 1)
                dve.wait_ge(setup_v, 11)
                V.tensor_scalar(om[:], dec[:], -1.0, 1.0, ALU.mult, ALU.add).then_inc(setup_v, 1)
                dve.wait_ge(setup_v, 12)
                V.scalar_tensor_tensor(omd2[:], dec[:], 1.0, om[:], ALU.add, ALU.mult).then_inc(decay_done, 1)
                dve.wait_ge(decay_done, 1)

            def cut(tile):
                b, l, ct = tile
                dve.wait_ge(k_in[ct], k_count(b, l))
                if (b, l) != (0, 0):
                    dve.wait_ge(ratio_done, s_of(b, l, ct) - 3)
                V.tensor_scalar(fd[:, ct, :], k_sb[:, ct, :], CLAMP, None, ALU.min).then_inc(kc_done, 1)
                V.tensor_scalar(eu[:, ct, :], k_sb[:, ct, :], wu[:, 1, l, ct:ct + 1], CLAMP, ALU.add, ALU.min).then_inc(kc_done, 1)

            def forward(tile):
                b, l, ct = tile
                d = col(dec, b, l, ct).broadcast_to([P, T])
                dve.wait_ge(ekv_done, s_of(b, l, ct) + 1)
                for f in (fd, fn):
                    V.tensor_tensor_scan(f[:, ct, :], d, f[:, ct, :], 0.0, ALU.mult, ALU.add).then_inc(fwd_done, 1)

            def backward(tile):
                b, l, ct = tile
                s = s_of(b, l, ct)
                d = col(dec, b, l, ct).broadcast_to([P, T - 1])
                for n, f in enumerate((fd, fn)):
                    dve.wait_ge(scaled_done, s * 2 + (n + 1))
                    back = f[:, ct, 0:T - 1][:, ::-1]
                    V.tensor_tensor_scan(back, d, back, f[:, ct, T - 1:T], ALU.mult, ALU.add).then_inc(bwd_done, 1)
                dve.wait_ge(bwd_done, s * 2 + 1)
                dve.wait_ge(exp_done, s * 2 + 2)
                V.tensor_tensor(fd[:, ct, :], fd[:, ct, :], eu[:, ct, :], ALU.add).then_inc(den_done, 1)

            def ratio(tile):
                b, l, ct = tile
                s = s_of(b, l, ct)
                dve.wait_ge(y_done, s + 1)
                dve.wait_ge(num_done, s + 1)
                if l == 1 and b > 0:
                    dve.wait_ge(c1lo_done, b * 4 + ct - 3)
                    dve.wait_ge(logits_done, group(b - 1, 1) + 1)
                dst = cond1[:, ct, :] if l else fn[:, ct, :]
                V.scalar_tensor_tensor(dst, fd[:, ct, :], 1.0 / DEN_MIN, fn[:, ct, :], ALU.min, ALU.mult).then_inc(ratio_done, 1)

            def cut_x(tile):
                b, l, ct = tile
                if l == 0:
                    dve.wait_ge(x_in, b * 16 + 16)
                else:
                    dve.wait_ge(acc_read, acc_count(b, 0, ct))
                s = sig_of(b, l, ct)
                if (b, l) in APART and ct >= 2:
                    if b > 0:
                        dve.wait_ge(lo_done, b * 8)
                elif s >= 2:
                    pb, pl = GROUPS[(s - 2) // CT]
                    dve.wait_ge(cond_done[pl], pb * CT + (s - 2) % CT + 1)
                V.tensor_scalar(sigma(b, l, ct), x_tile(b, ct), X_MIN, None, ALU.max).then_inc(xc_done, 1)

            def condition1(b, ct):
                dve.wait_ge(sig_done, sig_of(b, 1, ct) + 1)
                dve.wait_ge(ratio_done, s_of(b, 1, ct) + 1)
                V.tensor_tensor(cond1[:, ct, :], cond1[:, ct, :], sigma(b, 1, ct), ALU.mult).then_inc(cond_done[1], 1)

            def top2(b, l):
                z = group(b, l)
                n0 = z * SMALL

                def sync_to(n):
                    dve.wait_ge(small, n0 + n)

                dve.wait_ge(logits_done, z + 1)
                if l == 0:
                    V.tensor_copy(lg[:], lgp[0]).then_inc(small, 1)
                else:
                    dve.wait_ge(lnss_done, b + 1)
                    V.tensor_scalar(rn[:], rn[:], log(NORM_MIN ** 2 * SS_SCALE), None, ALU.max).then_inc(ssmax_done, 1)
                    dve.wait_ge(rn_done, b + 1)
                    V.tensor_tensor(lg[:], lgp[1], rn[:].unsqueeze(2).broadcast_to([P, TT, NE]), ALU.mult).then_inc(small, 1)
                sync_to(1)
                for t in range(TT):
                    last = V.max(mx[:, t, :], lg[:, t, :])
                last.then_inc(small, 1)
                sync_to(2)
                V.tensor_tensor(dlt[:], mx[:, :, 1], mx[:, :, 0], ALU.subtract).then_inc(small, 1)
                for t in range(TT):
                    last = V.max_index(mi[:, t, :], mx[:, t, :], lg[:, t, :])
                last.then_inc(small, 1)
                sync_to(4)
                V.tensor_copy(idxf[:], mi[:, :, 0:2]).then_inc(small, 1)
                dve.wait_ge(edl_done, z + 1)
                V.tensor_scalar(den2[:], edl[:], 1.0, None, ALU.add).then_inc(small, 1)
                sync_to(5)
                dve.wait_ge(consts_done, 3 + NE)
                V.tensor_tensor(oh[:], iota[:], idxf[:].unsqueeze(3).broadcast_to([P, TT, 2, NE]), ALU.is_equal).then_inc(small, 1)
                sync_to(6)
                V.reciprocal(rec2[:], den2[:]).then_inc(small, 1)
                sync_to(8)
                gain = ALPHA if l == 0 else 1.0
                V.tensor_scalar(wp[:, :, 0], rec2[:], gain, None, ALU.mult)
                V.scalar_tensor_tensor(wp[:, :, 1], edl[:], gain, rec2[:], ALU.mult, ALU.mult).then_inc(small, 1)
                sync_to(9)
                V.tensor_tensor(oh[:], oh[:], wp[:].unsqueeze(3).broadcast_to([P, TT, 2, NE]), ALU.mult).then_inc(small, 1)
                sync_to(10)
                if l == 0:
                    wide = (oh[:, :, j, :].unsqueeze(3).broadcast_to([P, TT, NE, RANK0]) for j in range(2))
                    V.tensor_tensor(lora_h[:].rearrange("p (t e r) -> p t e r", t=TT, e=NE), *wide, ALU.add).then_inc(cw_done, 1)
                else:
                    V.tensor_tensor(cw[:], oh[:, :, 0, :], oh[:, :, 1, :], ALU.add).then_inc(cw_done, 1)

            def weigh_lora(b):
                dve.wait_ge(lorah_done, b * 4 + 4)
                dve.wait_ge(wrep_evac, b + 1)
                V.tensor_tensor(lora_h[:], hb[:, 0, :], lora_h[:], ALU.mult).then_inc(lorah_used, 1)

            def end_ffn0(b, o):
                dve.wait_ge(ffn0_done, b * 4 + (o + 1))
                V.tensor_tensor(x_tile(b, o), acc[:, o, :], x_tile(b, o), ALU.add).then_inc(acc_read, 1)

            def residual0(b):
                for o in range(CT):
                    end_ffn0(b, o)

            def split_lo(f, ct):
                dve.wait_ge(c1hi_done, f * 4 + (ct + 1))
                V.tensor_tensor(cond1_lo[:, ct, :], cond1[:, ct, :], cond1_hi[:, ct, :].bitcast(F32), ALU.subtract).then_inc(c1lo_done, 1)

            def weigh(f, e):
                n = f * 8 + e
                dve.wait_ge(h_done, n + 1)
                if (f, e) in COMB_LOADS:
                    dve.wait_ge(comb_in[e % 4], comb_count(f, e))
                else:
                    dve.wait_ge(comb_copied, e + 1)
                if e >= 2:
                    dve.wait_ge(lo_done, n - 1)
                elif f > 0:
                    dve.wait_ge(acc_read, acc_count(f - 1, 1, 0))
                V.tensor_tensor(hs[:, e % 2, :], hb[:, (e + 2) % 3, :], comb[:, e % 4, :], ALU.mult).then_inc(hs_done, 1)

            def residual1(f):
                for o in range(CT):
                    dve.wait_ge(ffn1_done, f * 4 + (o + 1))
                    V.tensor_tensor(x_tile(f, o), acc[:, o, :], x_tile(f, o), ALU.add).then_inc(acc_read, 1)

            def tick_ahead(n, run):
                to_cut, to_scan = (tile_at(run, n + i) for i in (1, 0))
                if to_cut:
                    cut(to_cut)
                if to_scan:
                    forward(to_scan)

            def tick_back(n, run):
                to_return, to_divide = (tile_at(run, n + i) for i in (-1, -2))
                if to_return:
                    backward(to_return)
                    if not sig_apart(to_return):
                        cut_x(to_return)
                if to_divide and to_divide != (0, 1, CT - 1):
                    ratio(to_divide)
                    if to_divide[1] == 1 and not sig_apart(to_divide):
                        condition1(to_divide[0], to_divide[2])

            def tick(n, run):
                tick_ahead(n, run)
                tick_back(n, run)

            def ticks(run, first, end):
                for n in range(first, end):
                    tick(n, run)

            def late_start(b):
                for o in (0, 1):
                    end_ffn0(b, o)
                    cut_x((b, 1, o))

            def late_condition(b):
                for o in (2, 3):
                    end_ffn0(b, o)
                    cut_x((b, 1, o))
                condition1(b, 0)
                condition1(b, 1)
                if b == 0:
                    ratio((0, 1, CT - 1))
                add_square(dve, V, b, 1)
                condition1(b, 2)
                condition1(b, 3)
                split_lo(b, 0)
                add_square(dve, V, b, 2)
                split_lo(b, 1)
                split_lo(b, 2)
                add_square(dve, V, b, 3)
                split_lo(b, 3)

            dve.wait_ge(wu_in, 16)
            tick(-1, 0)
            decays()
            ticks(0, 0, 7)
            tick_ahead(7, 0)
            top2(0, 0)
            tick_back(7, 0)
            weigh_lora(0)
            tick_ahead(8, 0)
            late_start(0)
            tick_back(8, 0)
            late_condition(0)
            tick_ahead(9, 0)
            top2(0, 1)
            weights_lo(dve, V, 4)
            weights_lo(dve, V, 5)
            weigh(0, 0)
            tick_back(9, 0)
            tick_ahead(10, 0)
            weigh(0, 1)
            tick_back(10, 0)
            for n in range(11, 15):
                tick_ahead(n, 0)
                weigh(0, n - 9)
                tick_back(n, 0)
                if n - 5 < len(QUARTERS):
                    weights_lo(dve, V, n - 5)
            weigh(0, 6)
            tick_ahead(15, 0)
            weigh(0, 7)
            tick_back(15, 0)
            ticks(0, 16, 17)
            residual1(0)
            ticks(0, 17, 18)
            tick_ahead(18, 0)
            top2(1, 0)
            tick_back(18, 0)
            ticks(0, 19, 20)
            weigh_lora(1)
            ticks(0, 20, 22)
            late_start(1)
            late_condition(1)
            tick(-1, 1)
            top2(2, 0)
            tick(0, 1)
            top2(1, 1)
            weigh_lora(2)
            tick(1, 1)
            residual0(2)
            tick_ahead(2, 1)
            weigh(1, 0)
            tick_back(2, 1)
            weigh(1, 1)
            for n in range(2, 6):
                tick_ahead(n + 1, 1)
                weigh(1, n)
                tick_back(n + 1, 1)
            weigh(1, 6)
            tick_ahead(7, 1)
            weigh(1, 7)
            tick_back(7, 1)
            tick(8, 1)
            residual1(1)
            tick(9, 1)
            tick(-1, 2)
            for ct in range(CT):
                split_lo(2, ct)
            tick(0, 2)
            top2(3, 0)
            tick_ahead(1, 2)
            top2(2, 1)
            weigh_lora(3)
            tick_ahead(2, 2)
            residual0(3)
            tick_back(1, 2)
            weigh(2, 0)
            tick_back(2, 2)
            weigh(2, 1)
            for n in range(3, 6):
                tick_ahead(n, 2)
                weigh(2, n - 1)
                tick_back(n, 2)
            weigh(2, 5)
            top2(3, 1)
            weigh(2, 6)
            weigh(2, 7)
            for ct in range(CT):
                split_lo(3, ct)
            residual1(2)
            for e in range(NE):
                weigh(3, e)
            residual1(3)

        @block.scalar
        def _(act):
            A = nc.scalar.activation
            nc.scalar.preload_act_table_set("natural_log_exp_and_others")
            act.wait_ge(wu_in, 16)
            A(wu[:, 0], wu[:, 0], ACT.Exp).then_inc(setup_a, 1)
            act.wait_ge(setup_a, 1)
            A(wu[:, 0], wu[:, 0], ACT.Exp, scale=-1.0).then_inc(setup_a, 1)
            act.wait_ge(setup_v, 1)
            A(tf[:], tf[:], ACT.Exp, scale=-1.0).then_inc(setup_a, 1)

            def exps(tile):
                b, l, ct = tile
                for n, buf in enumerate((fd, eu)):
                    act.wait_ge(kc_done, s_of(b, l, ct) * 2 + (n + 1))
                    A(buf[:, ct, :], buf[:, ct, :], ACT.Exp).then_inc(exp_done, 1)

            def scale(tile):
                b, l, ct = tile
                for n, f in enumerate((fd, fn)):
                    act.wait_ge(fwd_done, s_of(b, l, ct) * 2 + (n + 1))
                    A(f[:, ct, 0:T - 1], f[:, ct, 0:T - 1], ACT.Copy, scale=col(omd2, b, l, ct)).then_inc(scaled_done, 1)

            def log_den(tile):
                b, l, ct = tile
                act.wait_ge(den_done, s_of(b, l, ct) + 1)
                A(fd[:, ct, :], fd[:, ct, :], ACT.Ln, bias=lntiny[:, 0:1]).then_inc(lnd_done, 1)

            def inverse_den(tile):
                b, l, ct = tile
                act.wait_ge(lnd_done, s_of(b, l, ct) + 1)
                A(fd[:, ct, :], fd[:, ct, :], ACT.Exp, scale=-1.0).then_inc(y_done, 1)

            def sigmoid(tile, step):
                b, l, ct = tile
                s, buf = sig_of(b, l, ct), sigma(b, l, ct)
                if step == 0:
                    act.wait_ge(xc_done, s + 1)
                    A(buf, buf, ACT.Exp, scale=-1.0).then_inc(sig_exp, 1)
                elif step == 1:
                    act.wait_ge(sig_exp, s + 1)
                    A(buf, buf, ACT.Ln, bias=1.0).then_inc(sig_ln, 1)
                else:
                    act.wait_ge(sig_ln, s + 1)
                    A(buf, buf, ACT.Exp, scale=-1.0, bias=ln_gain[:, b:b + 1]).then_inc(sig_done, 1)

            def tick_ahead(n, run):
                to_cut, to_scan = (tile_at(run, n + i) for i in (1, 0))
                if to_cut:
                    exps(to_cut)
                if to_scan:
                    scale(to_scan)

            def tick_back(n, run):
                to_return = tile_at(run, n - 1)
                if to_return is None:
                    return
                with_sig = not sig_apart(to_return)
                log_den(to_return)
                if with_sig:
                    sigmoid(to_return, 0)
                inverse_den(to_return)
                if with_sig:
                    sigmoid(to_return, 1)
                    sigmoid(to_return, 2)

            def tick(n, run):
                tick_ahead(n, run)
                tick_back(n, run)

            def ticks(run, first, end):
                for n in range(first, end):
                    tick(n, run)

            def edl_step(b, l):
                act.wait_ge(small, group(b, l) * SMALL + 3)
                A(edl[:], dlt[:], ACT.Exp).then_inc(edl_done, 1)

            def split_hi(f, ct):
                if f > 0:
                    act.wait_ge(h_done, f * 8)
                act.wait_ge(cond_done[1], f * 4 + ct + 1)
                A(cond1_hi[:, ct, :], cond1[:, ct, :], ACT.Copy).then_inc(c1hi_done, 1)

            def hi_part(f, e):
                n = f * 8 + e
                act.wait_ge(hs_done, n + 1)
                if e >= 2:
                    act.wait_ge(exp_out_done, f * 7 + e - 1)
                elif f > 0:
                    act.wait_ge(acc_read, acc_count(f - 1, 1, 0))
                A(hs_hi[:, e % 2, :], hs[:, e % 2, :], ACT.Copy).then_inc(hi_done, 1)

            def gates1(b):
                act.wait_ge(logits_done, group(b, 1) + 1)
                A(rn[:], ssp, ACT.Ln, scale=SS_SCALE, bias=lntiny[:, 0:1]).then_inc(lnss_done, 1)
                act.wait_ge(ssmax_done, b + 1)
                A(rn[:], rn[:], ACT.Exp, scale=-0.5, bias=lntiny[:, 1:2]).then_inc(rn_done, 1)
                edl_step(b, 1)

            def copy_spread_comb():
                for e in range(SPREAD):
                    act.wait_ge(comb_spread, e + 1)
                    A(comb[:, e, :], acc[:, 2 + e, :], ACT.Copy).then_inc(comb_copied, 1)

            def evac_combT(f):
                act.wait_ge(ct_done, f + 1)
                A(combT, hb[0:NE, 1, :], ACT.Copy).then_inc(ct_evac, 1)

            def weights_hi(n):
                which, c = QUARTERS[n]
                act.wait_ge(raw_in[which, c // 2], 16)
                hi = (wa_hi[:].rearrange("p e k r -> p (e k r)"), wb_hi[:].rearrange("p e o -> p (e o)"))[which]
                raw = stage[which, c // 2][:, c % 2 * QUARTER:(c % 2 + 1) * QUARTER]
                A(hi[:, c * QUARTER:(c + 1) * QUARTER], raw, ACT.Copy).then_inc(whi_done, 1)

            def square(b, ct):
                act.wait_ge(cond_done[1], b * 4 + ct + 1)
                if ct == 0:
                    if b > 0:
                        act.wait_ge(comb_out, b * 16)
                    A(ss[:], cond1[:, ct, :], ACT.Square).then_inc(squared, 1)
                    return
                if ct > 1:
                    act.wait_ge(sq_added, b * 3 + (ct - 1))
                A(sq[:], cond1[:, ct, :], ACT.Square).then_inc(squared, 1)

            def wrep_to_sbuf(b):
                act.wait_ge(wrep_done, b + 1)
                A(lora_h[:], hb[:, 1, :], ACT.Copy).then_inc(wrep_evac, 1)

            def late_sigmoids(b, *cts):
                for step in range(3):
                    for ct in cts:
                        sigmoid((b, 1, ct), step)

            def late_rest(b):
                late_sigmoids(b, 2, 3)
                split_hi(b, 0)
                split_hi(b, 1)
                square(b, 2)
                split_hi(b, 2)
                split_hi(b, 3)
                square(b, 3)

            tick(-1, 0)
            act.wait_ge(setup_v, 7)
            A(ln_gain[:], ln_gain[:], ACT.Ln).then_inc(setup_a, 1)
            act.wait_ge(setup_a, 4)
            act.wait_ge(decay_done, 1)
            for n in range(7):
                tick(n, 0)
            weights_hi(0)
            tick_ahead(7, 0)
            edl_step(0, 0)
            weights_hi(1)
            tick_back(7, 0)
            wrep_to_sbuf(0)
            weights_hi(2)
            tick_ahead(8, 0)
            late_sigmoids(0, 0, 1)
            tick_back(8, 0)
            late_rest(0)
            tick_ahead(9, 0)
            gates1(0)
            for n in (3, 4, 5):
                weights_hi(n)
            copy_spread_comb()
            evac_combT(0)
            hi_part(0, 0)
            tick_back(9, 0)
            tick_ahead(10, 0)
            hi_part(0, 1)
            tick_back(10, 0)
            for n in range(11, 15):
                if n - 5 < len(QUARTERS):
                    weights_hi(n - 5)
                tick_ahead(n, 0)
                hi_part(0, n - 9)
                tick_back(n, 0)
            hi_part(0, 6)
            tick_ahead(15, 0)
            hi_part(0, 7)
            tick_back(15, 0)
            ticks(0, 16, 17)
            ticks(0, 17, 18)
            tick_ahead(18, 0)
            edl_step(1, 0)
            tick_back(18, 0)
            tick_ahead(19, 0)
            wrep_to_sbuf(1)
            tick_back(19, 0)
            ticks(0, 20, 22)
            late_sigmoids(1, 0, 1)
            late_rest(1)
            tick(-1, 1)
            edl_step(2, 0)
            tick(0, 1)
            gates1(1)
            wrep_to_sbuf(2)
            tick_ahead(1, 1)
            evac_combT(1)
            tick_back(1, 1)
            tick_ahead(2, 1)
            hi_part(1, 0)
            tick_back(2, 1)
            hi_part(1, 1)
            for n in range(2, 6):
                tick_ahead(n + 1, 1)
                hi_part(1, n)
                tick_back(n + 1, 1)
            hi_part(1, 6)
            square(2, 0)
            tick_ahead(7, 1)
            hi_part(1, 7)
            tick_back(7, 1)
            square(2, 1)
            tick(8, 1)
            square(2, 2)
            tick(9, 1)
            square(2, 3)
            tick(-1, 2)
            for ct in range(CT):
                split_hi(2, ct)
            tick(0, 2)
            edl_step(3, 0)
            tick_ahead(1, 2)
            gates1(2)
            wrep_to_sbuf(3)
            tick_ahead(2, 2)
            evac_combT(2)
            tick_back(1, 2)
            hi_part(2, 0)
            tick_back(2, 2)
            square(3, 0)
            hi_part(2, 1)
            for n in range(3, 6):
                tick_ahead(n, 2)
                hi_part(2, n - 1)
                tick_back(n, 2)
                square(3, n - 2)
            hi_part(2, 5)
            gates1(3)
            hi_part(2, 6)
            evac_combT(3)
            hi_part(2, 7)
            for ct in range(CT):
                split_hi(3, ct)
            for e in range(NE):
                hi_part(3, e)

        @block.gpsimd
        def _(pool):
            G = nc.gpsimd
            G.memset(ident[:], 0.0).then_inc(consts_done, 1)
            pool.wait_ge(consts_done, 1)
            G.affine_select(out=ident[:], in_=ident[:], compare_op=ALU.not_equal, fill=1.0, base=0,
                            pattern=[[-1, P]], channel_multiplier=1).then_inc(consts_done, 1)
            G.memset(ones[:], 1.0).then_inc(consts_done, 1)
            for e in range(NE):
                G.memset(iota[:, :, :, e:e + 1], float(e)).then_inc(consts_done, 1)

            def ekv_step(tile):
                b, l, ct = tile
                s = s_of(b, l, ct)
                if s >= CT and WKV[s // CT - 1][1] == 0:
                    pool.wait_ge(cond_done[0], WKV[s // CT - 1][0] * CT + ct + 1)
                pool.wait_ge(exp_done, s * 2 + 1)
                G.tensor_tensor(fn[:, ct, :], fd[:, ct, :], k_sb[:, ct, :], ALU.mult).then_inc(ekv_done, 1)
                pool.wait_ge(exp_done, s * 2 + 2)
                pool.wait_ge(ekv_done, s + 1)
                G.tensor_tensor(ekuv(b, l, ct), eu[:, ct, :], k_sb[:, ct, :], ALU.mult).then_inc(g_done, 1)

            def numerator(tile):
                b, l, ct = tile
                s = s_of(b, l, ct)
                pool.wait_ge(g_done, s + 1)
                pool.wait_ge(bwd_done, s * 2 + 2)
                G.tensor_tensor(fn[:, ct, :], fn[:, ct, :], ekuv(b, l, ct), ALU.add).then_inc(num_done, 1)

            def condition0(b, ct):
                pool.wait_ge(sig_done, sig_of(b, 0, ct) + 1)
                pool.wait_ge(ratio_done, s_of(b, 0, ct) + 1)
                if b > 0:
                    pool.wait_ge(cond0_used, b * 4 + ct - 3)
                G.tensor_tensor(cond0[:, ct, :], fn[:, ct, :], sig[:, ct % 2, :], ALU.mult).then_inc(cond_done[0], 1)

            def tick_ahead(n, run):
                to_cut = tile_at(run, n + 1)
                if to_cut:
                    ekv_step(to_cut)

            def tick_back(n, run):
                to_return, to_divide = (tile_at(run, n + i) for i in (-1, -2))
                if to_return:
                    numerator(to_return)
                if to_divide and to_divide[1] == 0:
                    condition0(to_divide[0], to_divide[2])

            def tick(n, run):
                tick_ahead(n, run)
                tick_back(n, run)

            def ticks(run, first, end):
                for n in range(first, end):
                    tick(n, run)

            def lo_part(f, e):
                n = f * 8 + e
                pool.wait_ge(hi_done, n + 1)
                G.tensor_tensor(hs_lo[:, e % 2, :], hs[:, e % 2, :], hs_hi[:, e % 2, :].bitcast(F32), ALU.subtract).then_inc(lo_done, 1)

            def square(b, ct):
                pool.wait_ge(cond_done[1], b * 4 + ct + 1)
                if ct == 0 and b > 0:
                    pool.wait_ge(comb_out, b * 16)
                if ct > 1:
                    pool.wait_ge(sq_added, b * 3 + (ct - 1))
                G.tensor_tensor((sq if ct else ss)[:], cond1[:, ct, :], cond1[:, ct, :], ALU.mult).then_inc(squared, 1)

            for n in range(-1, 9):
                tick(n, 0)
                if n in (6, 7):
                    weights_lo(pool, G, n - 6)
            square(0, 0)
            square(0, 1)
            weights_lo(pool, G, 2)
            tick_ahead(9, 0)
            weights_lo(pool, G, 3)
            lo_part(0, 0)
            tick_back(9, 0)
            tick_ahead(10, 0)
            lo_part(0, 1)
            tick_back(10, 0)
            for n in range(11, 15):
                tick_ahead(n, 0)
                lo_part(0, n - 9)
                tick_back(n, 0)
            lo_part(0, 6)
            tick_ahead(15, 0)
            lo_part(0, 7)
            tick_back(15, 0)
            ticks(0, 16, 17)
            ticks(0, 17, 22)
            square(1, 0)
            square(1, 1)
            ticks(1, -1, 2)
            tick_ahead(2, 1)
            lo_part(1, 0)
            tick_back(2, 1)
            lo_part(1, 1)
            for n in range(2, 6):
                tick_ahead(n + 1, 1)
                lo_part(1, n)
                tick_back(n + 1, 1)
            lo_part(1, 6)
            tick_ahead(7, 1)
            lo_part(1, 7)
            tick_back(7, 1)
            add_square(pool, G, 2, 1)
            tick(8, 1)
            add_square(pool, G, 2, 2)
            tick(9, 1)
            add_square(pool, G, 2, 3)
            ticks(2, -1, 1)
            tick_ahead(1, 2)
            tick_ahead(2, 2)
            tick_back(1, 2)
            lo_part(2, 0)
            tick_back(2, 2)
            lo_part(2, 1)
            for n in range(3, 6):
                tick_ahead(n, 2)
                lo_part(2, n - 1)
                tick_back(n, 2)
                add_square(pool, G, 3, n - 2)
            lo_part(2, 5)
            lo_part(2, 6)
            lo_part(2, 7)
            for e in range(NE):
                lo_part(3, e)

        @block.tensor
        def _(pe):
            MM = nc.tensor.matmul
            pe.wait_ge(wf_in, 16 * 5)
            pe.wait_ge(consts_done, 3 + NE)

            def router1_logits(b, k):
                if k == 0 and b in (1, 2):
                    pe.wait_ge(small, group(b + 1, 0) * SMALL + 1)
                pe.wait_ge(cond_done[1], b * 4 + k + 1)
                for t in range(TT):
                    MM(lgp[1][:, t, :], cond1[:, k, t * P:(t + 1) * P], wrouter[:, k, :],
                       start=k == 0 and t == 0, stop=k == CT - 1, skip_group_check=True)

            def router1_norms(b):
                pe.wait_ge(sq_added, b * 3 + 3)
                for t in range(TT):
                    mm = MM(ssp[:, t:t + 1], ss[:, t * P:(t + 1) * P], ones[:, 0:1], start=True, stop=True)
                mm.then_inc(logits_done, 1)

            def lora_in(b, k):
                MM(hb[:, 0, :], wlora_a[:, k, :], cond0[:, k, :], start=k == 0, stop=k == CT - 1).then_inc(lorah_done, 1)

            def gate0_logits(b, t, k, start):
                mm = MM(lgp[0][:, t, :], cond0[:, k, t * P:(t + 1) * P], wgate[:, k, :], start=start, stop=k == CT - 1,
                        skip_group_check=True)
                if t == TT - 1 and k == CT - 1:
                    mm.then_inc(logits_done, 1)

            def ffn0_tile(b, k, gates):
                for o in range(CT):
                    gates(o)
                    if k == 0 and b > 0:
                        pe.wait_ge(acc_read, acc_before(b, 0, o))
                    mm = MM(acc[:, o, :], wffn[:, k, o * P:(o + 1) * P], cond0[:, k, :], start=k == 0, stop=False)
                mm.then_inc(cond0_used, 1)

            def no_gates(t):
                pass

            def lora_weights(b):
                pe.wait_ge(cw_done, group(b, 0) + 1)
                for t in range(TT):
                    mm = MM(hb[:, 1, t * P:(t + 1) * P], lora_h[:, t * P:(t + 1) * P], ident[:], start=True, stop=True)
                mm.then_inc(wrep_done, 1)

            def ffn0_arriving(b):
                for k in range(CT):
                    pe.wait_ge(cond_done[0], b * 4 + k + 1)
                    for t in range(TT):
                        gate0_logits(b, t, k, k == 0 and t == 0)
                    lora_in(b, k)
                    ffn0_tile(b, k, lambda o: lora_weights(b) if (k, o) == (CT - 1, 2) else None)

            def ffn0_gates_first(b):
                for k in range(CT):
                    pe.wait_ge(cond_done[0], b * 4 + k + 1)
                    lora_in(b, k)

                def gates(t):
                    for k in range(CT):
                        gate0_logits(b, t, k, k == 0)

                ffn0_tile(b, 0, gates)

            def lora_out(b):
                pe.wait_ge(lorah_used, b + 1)
                for o in range(CT):
                    MM(acc[:, o, :], wlora_b[:, o * P:(o + 1) * P], lora_h[:], start=False, stop=True).then_inc(ffn0_done, 1)

            def turn_comb(f):
                pe.wait_ge(cw_done, group(f, 1) + 1)
                if f in (1, 2):
                    pe.wait_ge(wrep_evac, f + 2)
                for t in range(TT):
                    mm = MM(hb[0:NE, 1, t * P:(t + 1) * P], cw[:, t, :], ident[:], start=True, stop=True)
                mm.then_inc(ct_done, 1)

            def spread_comb():
                pe.wait_ge(cw_done, group(0, 1) + 1)
                for e in range(SPREAD):
                    for t in range(TT):
                        mm = MM(acc[:, 2 + e, t * P:(t + 1) * P], cw[:, t, e:e + 1].broadcast_to([P, P]), ident[:],
                                start=True, stop=True)
                    mm.then_inc(comb_spread, 1)

            def wait_split(which, c):
                n = QUARTERS.index((which, c))
                pe.wait_ge(wlo_done[n // 4], n % 4 + 1)

            def hidden(f, e):
                if e == 2:
                    pe.wait_ge(ct_evac, f + 1)
                if f == 0:
                    wait_split(0, e // 2)
                n = 0
                for k in range(CT):
                    for w, c in ((wa_hi, cond1_hi), (wa_hi, cond1_lo), (wa_lo, cond1_hi)):
                        mm = MM(hb[:, (e + 2) % 3, :], w[:, e, k, :], c[:, k, :], start=n == 0, stop=n == 3 * CT - 1)
                        n += 1
                mm.then_inc(h_done, 1)

            def expert_out(f, e, between=no_gates):
                pe.wait_ge(lo_done, f * 8 + (e + 1))
                if f == 0:
                    wait_split(1, e // 2)
                for o in range(CT):
                    if e == 0:
                        pe.wait_ge(acc_read, acc_before(f, 1, o))
                        if f == 0 and o == 2:
                            pe.wait_ge(comb_copied, SPREAD)
                    for n, (w, h) in enumerate(((wb_hi, hs_hi), (wb_hi, hs_lo), (wb_lo, hs_hi))):
                        mm = MM(acc[:, o, :], w[:, e, o * P:(o + 1) * P], h[:, e % 2, :], start=e == 0 and n == 0,
                                stop=e == NE - 1 and n == 2)
                    between(o)
                    if e == NE - 1:
                        mm.then_inc(ffn1_done, 1)
                if e < NE - 1:
                    mm.then_inc(exp_out_done, 1)

            def ffn1_first(f):
                pe.wait_ge(c1lo_done, f * 4 + 4)
                hidden(f, 0)

            def ffn1_rest(f):
                hidden(f, 1)
                for e in range(NE):
                    if e + 2 < NE:
                        hidden(f, e + 2)
                    if f == 2 and e == 6:
                        turn_comb(3)
                    if f == 2 and e == 3:
                        expert_out(f, e, lambda o: router1_logits(3, o))
                    elif f == 2 and e == 4:
                        expert_out(f, e, lambda o: router1_norms(3) if o == 0 else None)
                    else:
                        expert_out(f, e)

            ffn0_arriving(0)
            lora_out(0)
            for k in range(CT):
                router1_logits(0, k)
            router1_norms(0)
            ffn1_first(0)
            spread_comb()
            turn_comb(0)
            ffn1_rest(0)

            ffn0_gates_first(1)
            for k in (1, 2):
                ffn0_tile(1, k, no_gates)
            lora_weights(1)
            ffn0_tile(1, 3, no_gates)
            lora_out(1)

            ffn0_gates_first(2)
            ffn0_tile(2, 1, no_gates)
            ffn0_tile(2, 2, lambda o: router1_logits(1, o))
            router1_norms(1)
            lora_weights(2)
            ffn0_tile(2, 3, no_gates)
            turn_comb(1)
            lora_out(2)
            ffn1_first(1)
            ffn1_rest(1)

            ffn0_gates_first(3)
            ffn0_tile(3, 1, no_gates)
            ffn0_tile(3, 2, lambda o: router1_logits(2, o))
            router1_norms(2)
            lora_weights(3)
            ffn0_tile(3, 3, no_gates)
            turn_comb(2)
            lora_out(3)
            ffn1_first(2)
            ffn1_rest(2)

            ffn1_first(3)
            ffn1_rest(3)


_SHAPES = {
    "xT": (B, P, CT, T), "kT": (B, CT, P, T), "cond": (1, B * P), "wu": (P, 2, 2, CT), "w_ffn0": (P, CT, C),
    "gate0": (P, CT, NE), "lora_a": (P, CT, P), "lora_b": (P, C), "router1": (P, CT, NE),
    "wa1": (P, NE * CT * P), "wb1": (P, NE * C),
}


def kernel(x, fside_BxSxS_0, cond_512, L0_cond_w, L0_cond_u, L0_ffn_W, L0_ffn_gate_w, L0_ffn_A, L0_ffn_B,
           L1_cond_w, L1_cond_u, L1_ffn_router_w, L1_ffn_Wa, L1_ffn_Wb):
    import numpy as np
    import concourse.bacc as bacc
    from concourse.bass_utils import run_bass_kernel_spmd

    def rows(w):
        return np.asarray(w).reshape(CT, P, -1).transpose(1, 0, 2)

    x, k = np.asarray(x), np.asarray(fside_BxSxS_0)
    wu = np.stack([np.asarray(a).reshape(CT, P) for a in (L0_cond_w, L1_cond_w, L0_cond_u, L1_cond_u)])
    data = {
        "xT": x.reshape(B, T, CT, P).transpose(0, 3, 2, 1),
        "kT": k.reshape(B, T, CT, P).transpose(0, 2, 3, 1),
        "cond": np.asarray(cond_512).reshape(1, B * P),
        "wu": wu.reshape(2, 2, CT, P).transpose(3, 0, 1, 2),
        "w_ffn0": rows(np.asarray(L0_ffn_W).T),
        "gate0": rows(np.asarray(L0_ffn_gate_w).T),
        "lora_a": rows(np.asarray(L0_ffn_A).reshape(P, C).T),
        "lora_b": np.asarray(L0_ffn_B).transpose(0, 2, 1).reshape(P, C),
        "router1": rows(L1_ffn_router_w),
        "wa1": np.asarray(L1_ffn_Wa).reshape(NE, CT, P, P).transpose(2, 0, 1, 3).reshape(P, -1),
        "wb1": np.asarray(L1_ffn_Wb).transpose(1, 0, 2).reshape(P, -1),
    }
    nc = bacc.Bacc("TRN2", target_bir_lowering=False, num_devices=1)
    arrays, args = {}, []
    for name, shape in _SHAPES.items():
        arrays[name + "_dram"] = np.ascontiguousarray(data[name])
        args.append(nc.dram_tensor(name + "_dram", shape, F32, kind="ExternalInput").ap())
    out = nc.dram_tensor("out_dram", (B, P, CT, T), F32, kind="ExternalOutput").ap()
    scratch = nc.dram_tensor("comb_dram", (2, NE, T), F32).ap()
    build(nc, *args, out, scratch)
    r = run_bass_kernel_spmd(nc, [arrays], core_ids=[0])
    got = np.asarray(r.results[0]["out_dram"])
    return np.ascontiguousarray(got.transpose(0, 3, 2, 1)).reshape(B, T, C)
```
